# Optimizing a Trainium2 kernel written in Bass

```python
import numpy as np
import jax
import jax.numpy as jnp

def _softmax(x, axis=-1):
    return jax.nn.softmax(x, axis=axis)

def _gelu(x):
    return jax.nn.gelu(x, approximate=True)

def _silu(x):
    return jax.nn.silu(x)

def _sigmoid(x):
    return jax.nn.sigmoid(x)

def _layernorm(x, axis=-1, eps=1e-05):
    m = jnp.mean(x, axis=axis, keepdims=True)
    v = jnp.var(x, axis=axis, keepdims=True)
    return (x - m) / jnp.sqrt(v + eps)

def _scatter_add(tgt, idx, src, axis=0):
    return tgt.at[idx].add(src)

def _segment_sum(src, seg, n):
    return jax.ops.segment_sum(src, seg, n)
kernel_name = 'mk_macaron_d1_jaxref_r8_14dc1d'

def setup_inputs(seed: int=0):
    np.random.seed(seed)
    _w = jnp.asarray

    def _L0_attn_setup():
        import jax, jax.numpy as jnp
        import numpy as np
        B, S, D, H = (4, 256, 128, 16)
        DH = D // H
        key = jax.random.key(seed)
        ks = jax.random.split(key, 9)
        sc = 0.02
        return {'x': jax.random.normal(ks[0], (B, S, D), jnp.float32), 'WQ': jax.random.normal(ks[1], (D, D), jnp.float32) * sc, 'bQ': jax.random.normal(ks[2], (D,), jnp.float32) * sc, 'WK': jax.random.normal(ks[3], (D, D), jnp.float32) * sc, 'bK': jax.random.normal(ks[4], (D,), jnp.float32) * sc, 'WV': jax.random.normal(ks[5], (D, D), jnp.float32) * sc, 'bV': jax.random.normal(ks[6], (D,), jnp.float32) * sc, 'WO': jax.random.normal(ks[7], (DH, D), jnp.float32) * sc, 'bO': jax.random.normal(ks[8], (D,), jnp.float32) * sc}
    _L0_attn_in = _L0_attn_setup()

    def _L0_ffn_setup():
        import jax, jax.numpy as jnp
        import numpy as np
        D_MODEL = 128
        EXPANSION = 4
        D_HIDDEN = D_MODEL * EXPANSION
        NUM_STAGES = int(np.log2(D_HIDDEN))

        def butterfly(y, weights, dim):
            lead = y.shape[:-1]
            for stage in range(weights.shape[0]):
                s = 2 ** stage
                nb = dim // (2 * s)
                yr = y.reshape(*lead, nb, 2, s)
                a = yr[..., 0, :]
                b = yr[..., 1, :]
                w = weights[stage].reshape(nb, s, 2, 2)
                na = w[..., 0, 0] * a + w[..., 0, 1] * b
                nb2 = w[..., 1, 0] * a + w[..., 1, 1] * b
                y = jnp.stack([na, nb2], axis=-2).reshape(*lead, dim)
            return y
        key = jax.random.key(seed)
        ks = jax.random.split(key, 6)
        B, S = (4, 256)
        x = jax.random.normal(ks[0], (B, S, D_MODEL), jnp.float32)
        W_exp = jax.random.normal(ks[1], (D_MODEL, D_HIDDEN), jnp.float32) * 0.02
        b_exp = jnp.zeros((D_HIDDEN,), jnp.float32)
        up_weights = jax.random.normal(ks[2], (NUM_STAGES, D_HIDDEN // 2, 2, 2), jnp.float32) * 0.02
        up_bias = jnp.zeros((D_HIDDEN,), jnp.float32)
        down_weights = jax.random.normal(ks[3], (NUM_STAGES, D_HIDDEN // 2, 2, 2), jnp.float32) * 0.02
        W_con = jax.random.normal(ks[4], (D_HIDDEN, D_MODEL), jnp.float32) * 0.02
        b_con = jnp.zeros((D_MODEL,), jnp.float32)
        down_bias = jnp.zeros((D_MODEL,), jnp.float32)
        return dict(x=x, W_exp=W_exp, b_exp=b_exp, up_weights=up_weights, up_bias=up_bias, down_weights=down_weights, W_con=W_con, b_con=b_con, down_bias=down_bias)
    _L0_ffn_in = _L0_ffn_setup()
    _d = {'L0_attn_x': _L0_attn_in['x'], 'L0_attn_WQ': _L0_attn_in['WQ'], 'L0_attn_bQ': _L0_attn_in['bQ'], 'L0_attn_WK': _L0_attn_in['WK'], 'L0_attn_bK': _L0_attn_in['bK'], 'L0_attn_WV': _L0_attn_in['WV'], 'L0_attn_bV': _L0_attn_in['bV'], 'L0_attn_WO': _L0_attn_in['WO'], 'L0_attn_bO': _L0_attn_in['bO'], 'L0_ffn_W_exp': _L0_ffn_in['W_exp'], 'L0_ffn_b_exp': _L0_ffn_in['b_exp'], 'L0_ffn_up_weights': _L0_ffn_in['up_weights'], 'L0_ffn_up_bias': _L0_ffn_in['up_bias'], 'L0_ffn_down_weights': _L0_ffn_in['down_weights'], 'L0_ffn_W_con': _L0_ffn_in['W_con'], 'L0_ffn_b_con': _L0_ffn_in['b_con'], 'L0_ffn_down_bias': _L0_ffn_in['down_bias']}
    _x0 = _d['L0_attn_x']
    _d['L0_attn_x'] = jax.random.normal(jax.random.fold_in(jax.random.key(seed), 1), (8, 256, 128), dtype=_x0.dtype)
    del _x0
    return _d

def reference(L0_attn_x, L0_attn_WQ, L0_attn_bQ, L0_attn_WK, L0_attn_bK, L0_attn_WV, L0_attn_bV, L0_attn_WO, L0_attn_bO, L0_ffn_W_exp, L0_ffn_b_exp, L0_ffn_up_weights, L0_ffn_up_bias, L0_ffn_down_weights, L0_ffn_W_con, L0_ffn_b_con, L0_ffn_down_bias):

    def _L0_attn_ref(x, WQ, bQ, WK, bK, WV, bV, WO, bO):
        import jax, jax.numpy as jnp
        import numpy as np
        B, S, D, H = (4, 256, 128, 16)
        DH = D // H
        b, s, d = x.shape
        h, dh = (H, DH)
        Q = (x @ WQ + bQ).reshape(b, s, h, dh).transpose(0, 2, 1, 3)
        K = (x @ WK + bK).reshape(b, s, h, dh).transpose(0, 2, 1, 3)
        V = (x @ WV + bV).reshape(b, s, h, dh).transpose(0, 2, 1, 3)
        scale = jnp.sqrt(jnp.float32(dh))
        scores = jnp.einsum('bhqd,bhkd->bhqk', Q, K) / scale
        causal = jnp.tril(jnp.ones((s, s), dtype=bool))
        scores = jnp.where(causal, scores, jnp.float32(-100000.0))
        A = jax.nn.softmax(scores, axis=-1)
        Z = jnp.einsum('bhqk,bhkd->bhqd', A, V)
        out = jnp.einsum('bhsd,de->bse', Z, WO) + jnp.float32(h) * bO
        return out

    def _L0_ffn_ref(x, W_exp, b_exp, up_weights, up_bias, down_weights, W_con, b_con, down_bias):
        import jax, jax.numpy as jnp
        import numpy as np
        D_MODEL = 128
        EXPANSION = 4
        D_HIDDEN = D_MODEL * EXPANSION
        NUM_STAGES = int(np.log2(D_HIDDEN))

        def butterfly(y, weights, dim):
            lead = y.shape[:-1]
            for stage in range(weights.shape[0]):
                s = 2 ** stage
                nb = dim // (2 * s)
                yr = y.reshape(*lead, nb, 2, s)
                a = yr[..., 0, :]
                b = yr[..., 1, :]
                w = weights[stage].reshape(nb, s, 2, 2)
                na = w[..., 0, 0] * a + w[..., 0, 1] * b
                nb2 = w[..., 1, 0] * a + w[..., 1, 1] * b
                y = jnp.stack([na, nb2], axis=-2).reshape(*lead, dim)
            return y
        h = jnp.einsum('bsd,dh->bsh', x, W_exp) + b_exp
        h = butterfly(h, up_weights, D_HIDDEN)
        h = jax.nn.gelu(h + up_bias, approximate=False)
        h = butterfly(h, down_weights, D_HIDDEN)
        y = jnp.einsum('bsh,hd->bsd', h, W_con) + b_con
        return y + down_bias
    x = L0_attn_x
    x = x + 0.5 * _L0_ffn_ref(_layernorm(x, axis=-1), L0_ffn_W_exp, L0_ffn_b_exp, L0_ffn_up_weights, L0_ffn_up_bias, L0_ffn_down_weights, L0_ffn_W_con, L0_ffn_b_con, L0_ffn_down_bias)
    x = x + _L0_attn_ref(_layernorm(x, axis=-1), L0_attn_WQ, L0_attn_bQ, L0_attn_WK, L0_attn_bK, L0_attn_WV, L0_attn_bV, L0_attn_WO, L0_attn_bO)
    x = x + 0.5 * _L0_ffn_ref(_layernorm(x, axis=-1), L0_ffn_W_exp, L0_ffn_b_exp, L0_ffn_up_weights, L0_ffn_up_bias, L0_ffn_down_weights, L0_ffn_W_con, L0_ffn_b_con, L0_ffn_down_bias)
    return x

_drawn_inputs = setup_inputs


def setup_inputs(seed=0):
    import zlib

    import numpy as np

    out = dict(_drawn_inputs(seed))
    spreads = {'L0_ffn_b_exp': (0.0, 0.1),
     'L0_ffn_up_bias': (0.0, 0.1),
     'L0_ffn_b_con': (0.0, 0.1),
     'L0_ffn_down_bias': (0.0, 0.1)}
    factors = {'L0_attn_WQ': 8.0,
     'L0_attn_bQ': 8.0,
     'L0_attn_WK': 8.0,
     'L0_attn_bK': 8.0,
     'L0_attn_WV': 6.655,
     'L0_attn_bV': 8.0,
     'L0_attn_WO': 6.997}
    for name, (base, spread) in spreads.items():
        noise = np.random.default_rng([zlib.crc32(name.encode()), seed]).standard_normal(out[name].shape)
        drawn = base * np.exp(spread * noise) if base else spread * noise
        out[name] = jnp.asarray(drawn.astype(out[name].dtype))
    for name, factor in factors.items():
        out[name] = (out[name] * factor).astype(out[name].dtype)
    return out
```

```python
import concourse.bass as bass
from concourse import mybir
from contextlib import ExitStack

F32 = mybir.dt.float32
BF16 = mybir.dt.bfloat16
ALU = mybir.AluOpType
ACT = mybir.ActivationFunctionType
AX = mybir.AxisListType

B, S, D, H = 8, 256, 128, 16
DH = D // H
HID = 4 * D
C = HID // D
STAGES = HID.bit_length() - 1
EPS = 1e-5
SCALE = float(DH) ** -0.5
MASKED = -1e30
HH = H // 2
HP = HH // 2
J = S // 64
UNITS = 2 * B
PARTS = 3
ROWS = PARTS * PARTS * DH
VW = 32

MAX_AT = {3: 0, 0: 256, 2: 320}
EXP_AT = {3: 0, 0: 64, 1: 320}


def build(nc, x, WQ, bQ, WK, bK, WV, bV, WO, bO, W_exp, b_exp, up_w, up_b, down_w, W_con, b_con, down_b, out):
    ctx = ExitStack()
    with ctx:
        def sb(name, shape, dt=F32):
            return ctx.enter_context(nc.sbuf_tensor(name, shape, dt))

        def sem(name):
            return ctx.enter_context(nc.semaphore(name))

        X = sb("X", [128, B, 2, D])
        HT = sb("HT", [128, B, C, S])
        XNT = sb("XNT", [128, B, S])
        XN = sb("XN", [128, 2, D])
        XN2T = sb("XN2T", [128, S])
        YS = sb("YS", [128, S])
        ST1 = sb("ST1", [128, 2 * B, 6])
        ST = sb("ST", [128, 2, 6])
        VE = sb("VE", [128, 2])
        MV1 = sb("MV1", [128, B, 2, 2])
        RS1 = sb("RS1", [128, B, 2])
        MV = sb("MV", [128, 2, 2])
        RS = sb("RS", [128, 2])
        POW = sb("POW", [128, B * 2])
        WUP = sb("WUP", [128, 2, HID])
        WDT = sb("WDT", [128, 2, HID])
        TM = sb("TM", [128, 2, HID])
        WDN = sb("WDN", [128, C, D])
        BW = sb("BW", [128, STAGES, 1024])
        WQs = sb("WQs", [128, D])
        WKs = sb("WKs", [128, D])
        WVs = sb("WVs", [128, D])
        WQP = sb("WQP", [128, D])
        WKP = sb("WKP", [128, D])
        WOs = sb("WOs", [DH + 1, D])
        BV = sb("BV", [128, D])
        BVP = sb("BVP", [128, D // 2])
        ROW = sb("ROW", [C, 2, D])
        RTM = sb("RTM", [C, 2, D])
        RW = sb("RW", [C, STAGES - 2, 256])
        RCOL = sb("RCOL", [8, D])
        COL = sb("COL", [128, 12])
        CW = sb("CW", [128, 2, 2, 4])
        CT = sb("CT", [128, 3, C])
        BUP = sb("BUP", [128, C])
        BQS = sb("BQS", [128, 1])
        BY = sb("BY", [128, 2])
        IDF = sb("IDF", [128, 128])
        IDB = sb("IDB", [128, 128], BF16)
        TRI = sb("TRI", [128, 2, 128])
        MSK = sb("MSK", [128, 2, 4, 64], BF16)
        QKF = sb("QKF", [128, 2, S])
        RES = sb("RES", [128, 2, S])
        PR = sb("PR", [128, 2, PARTS, S], BF16)
        VB = sb("VB", [128, H // 2, J, VW])
        QS = sb("QS", [128, 4, HH, S], BF16)
        KS = sb("KS", [128, 4, HH, S], BF16)
        VS = sb("VS", [128, 2, H // 2, J, VW])
        PX = sb("PX", [128, 2, 5, 512])
        PM = sb("PM", [128, 2, 5, 8])
        NM = sb("NM", [128, HP, J])
        NR = sb("NR", [128, HP * J])
        MP = sb("MP", [128, 8, HP * J], BF16)
        ZC = sb("ZC", [128, HP * J])
        EPSC = sb("EPSC", [128, 2])
        HOLD = sb("HOLD", [128, 1])
        MT = sb("MT", [PARTS * HP * J, 128], BF16)
        OT = sb("OT", [128, S])
        RD = sb("RD", [128, 2 * HH])
        ZH = sb("ZH", [128, 2, DH, H])
        Z = sb("Z", [128, 2, DH])
        ZT = sb("ZT", [DH + 1, S])
        P = [ctx.enter_context(nc.psum_tensor(f"P{i}", [128, 512], F32)) for i in range(8)]
        scr = nc.dram_tensor("scr", [B, 2, PARTS, DH, H, S], BF16).ap()
        scv = nc.dram_tensor("scv", [B, 128, H // 2 * J * VW], F32).ap()

        x_in = [sem(f"x_in{i}") for i in range(2)]
        w_in = sem("w_in")
        wup_in = sem("wup_in")
        wcon_in = sem("wcon_in")
        rcol_in = sem("rcol_in")
        cw_in = sem("cw_in")
        vb_const = sem("vb_const")
        wqk_ready = sem("wqk_ready")
        idb_ready = sem("idb_ready")
        dn_stage = sem("dn_stage")
        col_t = sem("col_t")
        xc1_ready = sem("xc1_ready")
        ve2_ready = sem("ve2_ready")
        ve3_ready = sem("ve3_ready")
        upw_in = [sem(f"upw_in{s}") for s in range(STAGES)]
        dnw_in = [sem(f"dnw_in{s}") for s in range(STAGES)]
        row_in = sem("row_in")
        const = sem("const")
        id_ready = sem("id_ready")
        tri_ready = sem("tri_ready")
        msk_ready = sem("msk_ready")
        dve_chain = sem("dve_chain")
        pool_chain = sem("pool_chain")
        ln1_stats = sem("ln1_stats")
        up_stage = sem("up_stage")
        wc_t = sem("wc_t")
        wdt_ready = sem("wdt_ready")
        wdn_t = sem("wdn_t")
        wdn_ready = sem("wdn_ready")
        row_folded = sem("row_folded")
        col_ready = sem("col_ready")
        bias_ready = sem("bias_ready")
        xn1_ready = sem("xn1_ready")
        t1_done = sem("t1_done")
        xnt1_ready = sem("xnt1_ready")
        up1_done = [sem(f"up1_done{c}") for c in range(C)]
        gelu1_done = [sem(f"gelu1_done{c}") for c in range(C)]
        down1_done = sem("down1_done")
        ys1_ready = sem("ys1_ready")
        yt1_done = sem("yt1_done")
        x1_done = sem("x1_done")
        st2 = sem("st2")
        mv2_ready = sem("mv2_ready")
        rs2_ready = sem("rs2_ready")
        xn2_ready = sem("xn2_ready")
        t2_done = sem("t2_done")
        xn2t_ready = sem("xn2t_ready")
        qk_done = sem("qk_done")
        v_done = sem("v_done")
        qkf_ready = sem("qkf_ready")
        part1_done = sem("part1_done")
        res_ready = sem("res_ready")
        part2_done = sem("part2_done")
        part3_done = sem("part3_done")
        vb_ready = sem("vb_ready")
        scr_out = sem("scr_out")
        scv_out = sem("scv_out")
        stack_in = [sem(f"stack_in{u}") for u in range(4)]
        v_in = [sem(f"v_in{u}") for u in range(2)]
        s1_done = [sem(f"s1_done{k}") for k in range(5)]
        max_done = [sem(f"max_done{k}") for k in range(5)]
        nm_ready = sem("nm_ready")
        mp1 = sem("mp1")
        mp2 = sem("mp2")
        mp3 = sem("mp3")
        mp_ready = sem("mp_ready")
        mt_done = sem("mt_done")
        mts_ready = sem("mts_ready")
        m_in = [sem(f"m_in{u}") for u in range(4)]
        s2_done = [sem(f"s2_done{k}") for k in range(5)]
        exp_done = [sem(f"exp_done{k}") for k in range(5)]
        pv_done = sem("pv_done")
        ot_ready = sem("ot_ready")
        ott_done = sem("ott_done")
        rd_ready = sem("rd_ready")
        zh_ready = sem("zh_ready")
        z_ready = sem("z_ready")
        zt_done = sem("zt_done")
        zts_ready = sem("zts_ready")
        wo_done = sem("wo_done")
        x2_done = sem("x2_done")
        st3 = sem("st3")
        mv3_ready = sem("mv3_ready")
        rs3_ready = sem("rs3_ready")
        xn3_ready = sem("xn3_ready")
        t3_done = sem("t3_done")
        xnt3_ready = sem("xnt3_ready")
        up3_done = [sem(f"up3_done{c}") for c in range(C)]
        gelu3_done = [sem(f"gelu3_done{c}") for c in range(C)]
        down3_done = sem("down3_done")
        ys3_ready = sem("ys3_ready")
        yt3_done = sem("yt3_done")
        out_ready = sem("out_ready")
        out_sent = sem("out_sent")

        CONSTS = 7
        up_flat = up_w.rearrange("s k a c -> s (k a c)")
        down_flat = down_w.rearrange("s k a c -> s (k a c)")

        FIRST, LAST = -2, UNITS + 1
        LOOP_FROM, ROUNDS = 3, 2

        def steps(eng, step):
            for s in range(FIRST, LOOP_FROM):
                step(s, s, 0)
            with eng.Fori(0, ROUNDS) as it:
                for s in range(LOOP_FROM, LOOP_FROM + 4):
                    step(s, it * 4 + s, it)
            for s in range(LOOP_FROM + 4 * ROUNDS, LAST + 1):
                step(s, s, 0)

        def one(b):
            return bass.ds(b, 1)

        def xb(b):
            return X[:, one(b), :, :].rearrange("p o u d -> p (o u) d")

        def bank(g, k):
            return (5 * g + k) % 2

        def head(par, hp):
            return HP * par + hp

        block = ctx.enter_context(nc.Block())

        @block.sync
        def _(sp):
            sp.dma_start(X[:, 0:4, :, :].rearrange("p b u d -> p (b u) d"),
                         x[0:4].rearrange("b (u p) d -> p (b u) d", p=128)).then_inc(x_in[0], 16)
            sp.dma_start(WUP[:, 0, :], W_exp).then_inc(wup_in, 16)
            sp.dma_start(X[:, 4:8, :, :].rearrange("p b u d -> p (b u) d"),
                         x[4:8].rearrange("b (u p) d -> p (b u) d", p=128)).then_inc(x_in[1], 16)
            for s in range(STAGES):
                sp.dma_start(BW[:, s, :], up_flat[s].partition_broadcast(128)).then_inc(upw_in[s], 16)
            for n in range(STAGES):
                sp.wait_ge(up_stage, n + 1)
                sp.dma_start(BW[:, n, :], down_flat[STAGES - 1 - n].partition_broadcast(128))\
                  .then_inc(dnw_in[n], 16)

            with sp.Fori(0, B) as b:
                sp.wait_ge(part3_done, b + 1)
                sp.dma_start(scr[one(b)].rearrange("o q r d h t -> (o d h) (q r) t"),
                             PR[:, :, :, :].rearrange("p q r t -> p (q r) t")).then_inc(scr_out, 16)
                sp.wait_ge(vb_ready, b + 1)
                sp.dma_start(scv[one(b)].rearrange("o p n -> (o p) n"),
                             VB[:, :, :, :].rearrange("p a b c -> p (a b c)")).then_inc(scv_out, 16)
            sp.wait_ge(scr_out, 16 * B)
            sp.wait_ge(scv_out, 16 * B)
            sp.wait_ge(const, CONSTS)

            def load_unit(u, b, half):
                heads = slice(half * HH, (half + 1) * HH)
                for i in range(PARTS):
                    src = scr[one(b), 0, i, :, heads, :].rearrange("o d h t -> o d (h t)")
                    sp.dma_start(QS[PARTS * DH * i:PARTS * DH * (i + 1), u, :, :]
                                 .rearrange("p h t -> p (h t)"),
                                 src.to_broadcast([PARTS, DH, HH * S])).then_inc(stack_in[u], 16)
                sp.dma_start(QS[ROWS:ROWS + PARTS, u, :, :], QS[ROWS + PARTS:ROWS + 2 * PARTS, u, :, :])\
                  .then_inc(stack_in[u], 16)
                src = scr[one(b), 1, :, :, heads, :].rearrange("o j d h t -> o (j d) (h t)")
                sp.dma_start(KS[0:ROWS, u, :, :].rearrange("p h t -> p (h t)"),
                             src.to_broadcast([PARTS, PARTS * DH, HH * S])).then_inc(stack_in[u], 16)

            def step(s, t, it):
                if s == FIRST:
                    load_unit(0, 0, 0)
                g = s + 3
                if g < UNITS:
                    if g >= 4:
                        sp.wait_ge(s2_done[4], t)
                    load_unit(g % 4, 2 * it + g // 2, g % 2)
                b = (s + 2) // 2
                if s % 2 == 0 and b < B:
                    if b >= 2:
                        sp.wait_ge(pv_done, t)
                    sp.dma_start(VS[:, b % 2, :, :, :].rearrange("p a b c -> p (a b c)"),
                                 scv[one(2 * it + b)].rearrange("o p n -> (o p) n")).then_inc(v_in[b % 2], 16)

            steps(sp, step)

            with sp.Fori(0, B) as b:
                sp.wait_ge(out_ready, b + 1)
                sp.dma_start(out[one(b)].rearrange("o (u p) d -> p (o u) d", p=128), xb(b))\
                  .then_inc(out_sent, 16)
            sp.wait_ge(out_sent, 16 * B)

        @block.gpsimd
        def _(pool):
            chain = [0]

            def link(ins):
                chain[0] += 1
                ins.then_inc(pool_chain, 1)
                pool.wait_ge(pool_chain, chain[0])

            link(pool.memset(IDF[:, :], 0.0))
            pool.affine_select(out=IDF[:, :], in_=IDF[:, :], compare_op=ALU.not_equal, fill=1.0, base=0,
                               pattern=[[-1, 128]], channel_multiplier=1).then_inc(id_ready, 1)
            pool.memset(POW[:, :], -0.5).then_inc(const, 1)
            pool.memset(EPSC[:, :], EPS).then_inc(const, 1)

            pool.wait_ge(row_in, 32)
            for s in range(STAGES - 2):
                w = 2 ** s
                y = ROW[:, s % 2, :].rearrange("p (n a w) -> p n a w", a=2, w=w)
                W = RW[:, s, :].rearrange("p (n w a c) -> p n w a c", w=w, a=2, c=2)
                for i in range(2):
                    ins = pool.tensor_tensor(RTM[:, i, :].rearrange("p (n a w) -> p n a w", a=2, w=w),
                                             W[:, :, :, :, i].rearrange("p n w a -> p n a w"),
                                             y[:, :, i:i + 1, :].to_broadcast([C, D // (2 * w), 2, w]), ALU.mult)
                link(ins)
                ins = pool.tensor_tensor(ROW[:, (s + 1) % 2, :], RTM[:, 0, :], RTM[:, 1, :], ALU.add)
                if s < STAGES - 3:
                    link(ins)
            ins.then_inc(row_folded, 1)

            pool.wait_ge(col_ready, 1)
            pool.wait_ge(cw_in, 32)
            for i in range(2):
                ins = pool.tensor_tensor(
                    CT[:, i, :].rearrange("p (n a) -> p n a", a=2), CW[:, 0, :, :]
                    .rearrange("p n (a c) -> p n a c", c=2)[:, :, :, i],
                    COL[:, 0:C].rearrange("p (n c) -> p n c", c=2)[:, :, i:i + 1].to_broadcast([128, 2, 2]), ALU.mult)
            link(ins)
            link(pool.tensor_tensor(CT[:, 2, :], CT[:, 0, :], CT[:, 1, :], ALU.add))
            for i in range(2):
                ins = pool.tensor_tensor(
                    CT[:, i, :].rearrange("p (a n) -> p n a", a=2), CW[:, 1, :, :]
                    .rearrange("p n (a c) -> p n a c", c=2)[:, :, :, i],
                    CT[:, 2, :].rearrange("p (c n) -> p n c", c=2)[:, :, i:i + 1].to_broadcast([128, 2, 2]), ALU.mult)
            link(ins)
            link(pool.tensor_tensor(CT[:, 2, :], CT[:, 0, :], CT[:, 1, :], ALU.add))
            pool.tensor_tensor(BUP[:, :], CT[:, 2, :], COL[:, 4:8], ALU.add).then_inc(bias_ready, 1)
            pool.tensor_scalar(BQS[:, :], COL[:, 8:9], SCALE, None, ALU.mult).then_inc(bias_ready, 1)
            link(pool.tensor_tensor(BY[:, 0:1], COL[:, 10:11], COL[:, 11:12], ALU.add))
            pool.tensor_scalar(BY[:, 1:2], BY[:, 0:1], 0.5, None, ALU.mult).then_inc(bias_ready, 1)

            pool.wait_ge(ln1_stats, 1)
            link(pool.tensor_scalar(MV1[:, :, :, 1], MV1[:, :, :, 1], EPS, None, ALU.add))
            link(pool.tensor_tensor(RS1[:, :, :].rearrange("p b u -> p (b u)"),
                                    MV1[:, :, :, 1].rearrange("p b u -> p (b u)"), POW[:, :], ALU.pow))

            def xn1(b):
                pool.tensor_tensor(XN[:, :, :], xb(b), MV1[:, one(b), :, 0:1]
                                   .rearrange("p o u c -> p (o u) c").to_broadcast([128, 2, D]),
                                   ALU.subtract).then_inc(xc1_ready, 1)
                pool.wait_ge(xc1_ready, b + 1)
                pool.tensor_tensor(XN[:, :, :], XN[:, :, :], RS1[:, one(b), :]
                                   .rearrange("p o u -> p (o u)").unsqueeze(2).to_broadcast([128, 2, D]),
                                   ALU.mult).then_inc(xn1_ready, 1)

            xn1(0)
            with pool.Fori(1, B) as b:
                pool.wait_ge(t1_done, b)
                xn1(b)

            link(pool.memset(TRI[:, :, :], 0.0))
            pool.affine_select(out=TRI[:, 0, :], in_=TRI[:, 0, :], compare_op=ALU.is_ge, fill=MASKED,
                               base=0, pattern=[[-1, 128]], channel_multiplier=1).then_inc(tri_ready, 1)
            pool.affine_select(out=TRI[:, 1, :], in_=TRI[:, 1, :], compare_op=ALU.is_ge, fill=MASKED,
                               base=0, pattern=[[1, 128]], channel_multiplier=-1).then_inc(tri_ready, 1)
            pool.memset(ZC[:, :], 0.0).then_inc(const, 1)
            pool.memset(MP[:, :, :], 0.0).then_inc(const, 1)
            pool.memset(KS[:, :, :, :], 1.0).then_inc(const, 1)
            pool.memset(QS[:, :, :, :], 0.0).then_inc(const, 1)
            pool.memset(ZT[:, :], float(H)).then_inc(const, 1)

            def rstd2(b):
                pool.wait_ge(mv2_ready, b + 1)
                pool.tensor_tensor(VE[:, :], MV[:, :, 1], EPSC[:, :], ALU.add).then_inc(ve2_ready, 1)
                pool.wait_ge(ve2_ready, b + 1)
                pool.tensor_tensor(RS[:, :], VE[:, :], POW[:, 0:2], ALU.pow).then_inc(rs2_ready, 1)

            def residue(b):
                pool.wait_ge(part1_done, b + 1)
                pool.tensor_tensor(RES[:, :, :], QKF[:, :, :], PR[:, :, 0, :], ALU.subtract)\
                    .then_inc(res_ready, 1)

            rstd2(0)
            with pool.Fori(0, B - 1) as b:
                rstd2(b + 1)
                residue(b)
            residue(B - 1)

            def step(s, t, it):
                g = s + 2
                if 0 <= g < UNITS:
                    nm = NM[:, :, :].rearrange("p a j -> p (a j)")
                    pool.wait_ge(nm_ready, t + 3)
                    if g >= 1:
                        pool.wait_ge(mt_done, t + 2)
                    pool.tensor_tensor(MP[:, 0, :], nm, ZC[:, :], ALU.add).then_inc(mp1, 1)
                    pool.wait_ge(mp1, t + 3)
                    pool.tensor_tensor(NR[:, :], nm, MP[:, 0, :], ALU.subtract).then_inc(mp2, 1)
                    pool.wait_ge(mp2, t + 3)
                    pool.tensor_tensor(MP[:, 1, :], NR[:, :], ZC[:, :], ALU.add).then_inc(mp3, 1)
                    pool.wait_ge(mp3, t + 3)
                    pool.tensor_tensor(MP[:, 2, :], NR[:, :], MP[:, 1, :], ALU.subtract).then_inc(mp_ready, 1)

            steps(pool, step)

            with pool.Fori(0, B) as b:
                pool.wait_ge(mv3_ready, b + 1)
                pool.tensor_tensor(VE[:, :], MV[:, :, 1], EPSC[:, :], ALU.add).then_inc(ve3_ready, 1)
                pool.wait_ge(ve3_ready, b + 1)
                pool.tensor_tensor(RS[:, :], VE[:, :], POW[:, 0:2], ALU.pow).then_inc(rs3_ready, 1)

        @block.scalar
        def _(act):
            act.dma_start(ROW[:, 0, :], b_exp.rearrange("(c n) -> c n", c=C)).then_inc(row_in, 16)
            act.dma_start(RW[:, :, :], up_flat[0:STAGES - 2].rearrange("s (c n) -> c s n", c=C))\
                .then_inc(row_in, 16)
            act.dma_start(WDN[:, :, :], W_con.rearrange("(c p) e -> p c e", p=128)).then_inc(wcon_in, 16)
            act.dma_start(RCOL[0:C, :], up_b.rearrange("(c n) -> c n", c=C)).then_inc(rcol_in, 16)
            for n, v in ((4, bQ), (5, bK)):
                act.dma_start(RCOL[n:n + 1, :].rearrange("o (d h) -> o d h", h=H),
                              v.rearrange("(o h d) -> o d h", o=1, h=H),
                               allow_slow_non_contiguous=True).then_inc(rcol_in, 16)
            for n, v in ((6, b_con), (7, down_b)):
                act.dma_start(RCOL[n:n + 1, :], v.rearrange("(o n) -> o n", o=1)).then_inc(rcol_in, 16)
            for m in range(2):
                act.dma_start(CW[:, m, :, :], up_w[STAGES - 2 + m].rearrange("(n p) a c -> p n (a c)", p=128))\
                    .then_inc(cw_in, 16)
            for w, of in ((WQs[:, :], WQ), (WKs[:, :], WK), (WVs[:, :], WV), (WOs[0:DH, :], WO),
                          (WOs[DH:DH + 1, :], bO.rearrange("(o n) -> o n", o=1)),
                          (BV[:, :], bV.partition_broadcast(128))):
                act.dma_start(w, of).then_inc(w_in, 16)

            act.wait_ge(wc_t, 1)
            act.activation(WDT[:, 0, :], P[7][:, :], ACT.Copy).then_inc(wdt_ready, 1)
            act.wait_ge(col_t, 1)
            act.activation(COL[:, 0:12], P[6][:, 0:12], ACT.Copy).then_inc(col_ready, 1)

            act.activation(IDB[:, :], IDF[:, :], ACT.Copy).then_inc(idb_ready, 1)
            act.wait_ge(w_in, 16 * 6)
            for dst, w in ((WQP, WQs), (WKP, WKs)):
                act.activation(dst[:, :].rearrange("k (d h) -> k d h", h=H),
                               w[:, :].rearrange("k (h d) -> k d h", h=H), ACT.Copy).then_inc(wqk_ready, 1)

            def gelu(b, c, up_done, gelu_done):
                act.wait_ge(up_done[c], b + 1)
                act.activation(HT[:, one(b), c, :].rearrange("p o t -> p (o t)"), P[1 + c][:, 0:S],
                               ACT.Gelu, bias=BUP[:, c:c + 1]).then_inc(gelu_done[c], 1)

            def xnt(b, t_done, ready):
                act.wait_ge(t_done, b + 1)
                act.activation(XNT[:, one(b), :].rearrange("p o t -> p (o t)"), P[0][:, 0:S], ACT.Copy)\
                   .then_inc(ready, 1)

            def ys(b, down_done, ready):
                act.wait_ge(down_done, b + 1)
                act.activation(YS[:, :], P[5][:, 0:S], ACT.Identity, bias=BY[:, 1:2], scale=0.5)\
                   .then_inc(ready, 1)

            xnt(0, t1_done, xnt1_ready)
            act.wait_ge(bias_ready, 3)

            def gelus1(b):
                gelu(b, 0, up1_done, gelu1_done)
                gelu(b, 1, up1_done, gelu1_done)
                xnt(b + 1, t1_done, xnt1_ready)
                gelu(b, 2, up1_done, gelu1_done)
                gelu(b, 3, up1_done, gelu1_done)

            gelus1(0)
            with act.Fori(1, B - 1) as b:
                gelus1(b)
            for c in range(C):
                gelu(B - 1, c, up1_done, gelu1_done)

            def ys1(b, first=False):
                if not first:
                    act.wait_ge(yt1_done, b)
                ys(b, down1_done, ys1_ready)

            def xn2t(b, first=False):
                if not first:
                    act.wait_ge(v_done, b)
                act.wait_ge(t2_done, b + 1)
                act.activation(XN2T[:, :], P[0][:, 0:S], ACT.Copy).then_inc(xn2t_ready, 1)

            def qk(b, first=False):
                if not first:
                    act.wait_ge(res_ready, b)
                    act.wait_ge(scr_out, b * 16)
                act.wait_ge(qk_done, b + 1)
                for n, (bias, scale) in enumerate(((BQS[:, :], SCALE), (COL[:, 9:10], 1.0))):
                    for dst in (QKF[:, n, :], PR[:, n, 0, :]):
                        ins = act.activation(dst, P[7][:, n * S:(n + 1) * S], ACT.Identity,
                                             bias=bias, scale=scale)
                ins.then_inc(part1_done, 1)

            ys1(0, True)
            ys1(1)
            xn2t(0, True)
            qk(0, True)
            with act.Fori(1, B - 1) as b:
                ys1(b + 1)
                xn2t(b)
                qk(b)
            xn2t(B - 1)
            qk(B - 1)

            act.wait_ge(tri_ready, 2)
            for par in range(2):
                rows = slice(64 * par, 64 * par + 64)
                for m in range(2):
                    act.activation(MSK[rows, m, :, :], TRI[rows, m, 64 * par:64 * par + 64].unsqueeze(1)
                                   .to_broadcast([64, 4, 64]), ACT.Copy).then_inc(msk_ready, 1)

            def exps(g, k, t):
                act.wait_ge(s2_done[k], t)
                act.activation(PX[:, g % 2, k, :], P[2 + bank(g, k)][:, :], ACT.Exp).then_inc(exp_done[k], 1)

            def step(s, t, it):
                if 0 <= s < UNITS:
                    if s >= 2:
                        act.wait_ge(pv_done, t - 1)
                    exps(s, 0, t + 1)
                g = s + 1
                if 0 <= g < UNITS:
                    act.wait_ge(mt_done, t + 2)
                    if g >= 1:
                        act.wait_ge(m_in[s % 4], (it + (s // 4 + 1)) * 32)
                    act.activation(MT[:, :], P[5][0:PARTS * HP * J, 0:64].bitcast(BF16), ACT.Copy)\
                       .then_inc(mts_ready, 1)
                    act.wait_ge(mts_ready, t + 2)
                    for par in range(2):
                        act.dma_start(QS[ROWS:ROWS + PARTS, g % 4, HP * par:HP * (par + 1), :]
                                      .rearrange("i h t -> i (h t)"),
                                      MT[:, 64 * par:64 * par + 64]).then_inc(m_in[g % 4], 16)
                if 0 <= s < UNITS:
                    exps(s, 1, t + 1)
                    exps(s, 2, t + 1)
                if 0 <= s - 1 < UNITS:
                    act.wait_ge(pv_done, t)
                    if s >= 2:
                        act.wait_ge(ott_done, t - 1)
                    act.activation(OT[:, :], P[4][:, 0:S], ACT.Copy).then_inc(ot_ready, 1)
                if 0 <= s < UNITS:
                    exps(s, 3, t + 1)
                b = (s - 3) // 2
                if s % 2 and 0 <= b < B:
                    act.wait_ge(zt_done, 2 * it + (b + 1))
                    if b >= 1:
                        act.wait_ge(wo_done, 2 * it + b)
                    act.activation(ZT[0:DH, :], P[7][0:DH, 0:S], ACT.Copy).then_inc(zts_ready, 1)
                if 0 <= s < UNITS:
                    exps(s, 4, t + 1)

            steps(act, step)

            def ys3(b, first=False):
                if not first:
                    act.wait_ge(yt3_done, b)
                ys(b, down3_done, ys3_ready)

            def ffn2(b, n):
                if n < B:
                    gelu(b, 0, up3_done, gelu3_done)
                    gelu(b, 1, up3_done, gelu3_done)
                if n + 1 < B:
                    xnt(b + 1, t3_done, xnt3_ready)
                if n < B:
                    gelu(b, 2, up3_done, gelu3_done)
                    gelu(b, 3, up3_done, gelu3_done)
                if 0 <= n - 1 < B:
                    ys3(b - 1, n == 1)

            xnt(0, t3_done, xnt3_ready)
            ffn2(0, 0)
            ffn2(1, 1)
            with act.Fori(2, B - 1) as b:
                ffn2(b, 2)
            for n in range(B - 1, B + 1):
                ffn2(n, n)

        @block.vector
        def _(dve):
            chain = [0]

            def link(ins):
                chain[0] += 1
                ins.then_inc(dve_chain, 1)
                dve.wait_ge(dve_chain, chain[0])

            for n in range(2 * B):
                if n % B == 0:
                    dve.wait_ge(x_in[n // B], 16)
                ins = dve.bn_stats(ST1[:, n, :], X[:, n // 2, n % 2, :])
            link(ins)
            for n in range(2 * B):
                ins = dve.bn_aggr(MV1[:, n // 2, n % 2, :], ST1[:, n, :])
            ins.then_inc(ln1_stats, 1)

            def stage(W, y, o, w, transposed, done):
                yv = y.rearrange("p (n a w) -> p n a w", a=2, w=w)
                Wv = W.rearrange("p (n w a c) -> p n w a c", w=w, a=2, c=2)
                for i in range(2):
                    wv = Wv[:, :, :, :, i].rearrange("p n w a -> p n a w") if not transposed else \
                        Wv[:, :, :, i, :].rearrange("p n w a -> p n a w")
                    ins = dve.tensor_tensor(TM[:, i, :].rearrange("p (n a w) -> p n a w", a=2, w=w), wv,
                                            yv[:, :, i:i + 1, :].to_broadcast([128, HID // (2 * w), 2, w]), ALU.mult)
                link(ins)
                ins = dve.tensor_tensor(o, TM[:, 0, :], TM[:, 1, :], ALU.add)
                done(ins)

            dve.wait_ge(wup_in, 16)
            for s in range(STAGES):
                dve.wait_ge(upw_in[s], 16)

                def done(ins):
                    ins.then_inc(up_stage, 1)
                    dve.wait_ge(up_stage, s + 1)
                stage(BW[:, s, :], WUP[:, s % 2, :], WUP[:, (s + 1) % 2, :], 2 ** s, False, done)
            dve.wait_ge(wdt_ready, 1)
            for n in range(STAGES):
                dve.wait_ge(dnw_in[n], 16)

                def done(ins):
                    ins.then_inc(dn_stage, 1)
                    dve.wait_ge(dn_stage, n + 1)
                stage(BW[:, n, :], WDT[:, n % 2, :], WDT[:, (n + 1) % 2, :], 2 ** (STAGES - 1 - n), True, done)
            dve.wait_ge(wdn_t, 1)
            dve.tensor_copy(WDN[:, :, :].rearrange("p c e -> p (c e)"), P[7][:, :]).then_inc(wdn_ready, 1)

            link(dve.memset(VB[:, :, :, :], 0.0))
            dve.memset(VB[0:64, :, :, DH:DH + 1], 1.0).then_inc(vb_const, 1)
            dve.memset(VB[64:128, :, :, VW // 2 + DH:VW // 2 + DH + 1], 1.0).then_inc(vb_const, 1)
            dve.wait_ge(vb_const, 2)
            dve.wait_ge(w_in, 16 * 6)

            def stats(b, st_done, mv_done, first):
                for u in range(2):
                    ins = dve.bn_stats(ST[:, u, :], X[:, one(b), u, :].rearrange("p o d -> p (o d)"))
                ins.then_inc(st_done, 1)
                dve.wait_ge(st_done, b + 1)
                dve.memset(HOLD[:, :], 0.0)
                for u in range(2):
                    ins = dve.bn_aggr(MV[:, u, :], ST[:, u, :])
                ins.then_inc(mv_done, 1)

            def normalise(b, rs_ready, left, ready, first):
                if not first:
                    dve.wait_ge(left, b)
                dve.wait_ge(rs_ready, b + 1)
                for u in range(2):
                    ins = dve.tensor_scalar(XN[:, u, :], X[:, one(b), u, :].rearrange("p o d -> p (o d)"),
                                            MV[:, u, 0:1], RS[:, u:u + 1], ALU.subtract, ALU.mult)
                ins.then_inc(ready, 1)

            def x1_stats(b, first=False):
                dve.wait_ge(yt1_done, b + 1)
                dve.tensor_tensor(xb(b), xb(b), P[6][:, 0:S].rearrange("p (u d) -> p u d", u=2), ALU.add)\
                   .then_inc(x1_done, 1)
                dve.wait_ge(x1_done, b + 1)
                dve.memset(HOLD[:, :], 0.0)
                stats(b, st2, mv2_ready, first)

            def v_blocks(b, first=False):
                if not first:
                    dve.wait_ge(scv_out, b * 16)
                dve.wait_ge(v_done, b + 1)
                for par in range(2):
                    rows = slice(64 * par, 64 * par + 64)
                    at = VW // 2 * par
                    ins = dve.tensor_tensor(
                        VB[rows, :, :, at:at + DH],
                        P[1][rows, 0:S].rearrange("p (j a d) -> p a j d", j=J, d=DH),
                        BVP[rows, :].rearrange("p (a d) -> p a d", d=DH).unsqueeze(2)
                        .to_broadcast([64, H // 2, J, DH]), ALU.add)
                ins.then_inc(vb_ready, 1)

            def parts(b):
                dve.wait_ge(res_ready, b + 1)
                dve.tensor_copy(PR[:, :, 1, :], RES[:, :, :]).then_inc(part2_done, 1)
                dve.wait_ge(part2_done, b + 1)
                dve.tensor_tensor(PR[:, :, 2, :], RES[:, :, :], PR[:, :, 1, :], ALU.subtract)\
                   .then_inc(part3_done, 1)

            for par in range(2):
                rows = slice(64 * par, 64 * par + 64)
                ins = dve.tensor_copy(
                    BVP[rows, :].rearrange("p (f n) -> p f n", f=2),
                    BV[rows, :].rearrange("p (f c n) -> p f c n", f=2, c=2)[:, :, par, :])
            link(ins)

            x1_stats(0, True)
            normalise(0, rs2_ready, t2_done, xn2_ready, True)
            x1_stats(1)
            v_blocks(0, True)
            normalise(1, rs2_ready, t2_done, xn2_ready, False)
            parts(0)
            with dve.Fori(1, B - 1) as b:
                x1_stats(b + 1)
                v_blocks(b)
                normalise(b + 1, rs2_ready, t2_done, xn2_ready, False)
                parts(b)
            v_blocks(B - 1)
            parts(B - 1)

            def maxima(g, k, t):
                dve.wait_ge(s1_done[k], t)
                dve.tensor_reduce(PM[:, g % 2, k, :], P[bank(g, k)][:, :].rearrange("p (n w) -> p n w", w=64),
                                  AX.X, ALU.max).then_inc(max_done[k], 1)

            def step(s, t, it):
                g = s + 2
                if 0 <= g < UNITS:
                    for k in range(5):
                        maxima(g, k, t + 3)
                    if g >= 1:
                        dve.wait_ge(mp2, t + 2)
                    dve.wait_ge(max_done[4], t + 3)
                    pm = PM[:, g % 2, :, :]
                    for j, of in ((3, pm[:, 0:HP, 0:4]), (0, pm[:, 0:HP, 4:5]), (2, pm[:, 0:HP, 5:8]),
                                  (1, pm[:, HP, :].rearrange("p (a j) -> p a j", j=2))):
                        ins = dve.tensor_reduce(NM[:, :, j], of, AX.X, ALU.max, negate=True)
                    ins.then_inc(nm_ready, 1)
                g = s - 1
                if 0 <= g < UNITS:
                    dve.wait_ge(ott_done, t)
                    o = P[6][:, 0:2 * 128].rearrange("p (n w) -> p n w", w=VW // 2)
                    dve.reciprocal(RD[:, :], o[:, :, DH]).then_inc(rd_ready, 1)
                    dve.wait_ge(rd_ready, t)
                    at = HH * (g % 2)
                    dve.tensor_tensor(ZH[:, :, :, at:at + HH].rearrange("p u d h -> p u h d"),
                                      P[6][:, 0:2 * 128].rearrange("p (u h w) -> p u h w", u=2, w=VW // 2)[:, :, :, 0:DH],
                                      RD[:, :].rearrange("p (u h) -> p u h", u=2).unsqueeze(3)
                                      .to_broadcast([128, 2, HH, DH]), ALU.mult).then_inc(zh_ready, 1)
                    if g % 2:
                        dve.wait_ge(zh_ready, t)
                        if g >= 2:
                            dve.wait_ge(zt_done, 2 * it + g // 2)
                        dve.tensor_reduce(Z[:, :, :].rearrange("p u d -> p (u d)"),
                                          ZH[:, :, :, :].rearrange("p u d h -> p (u d) h"),
                                          AX.X, ALU.add).then_inc(z_ready, 1)
                b = (s - 3) // 2
                if s % 2 and 0 <= b < B:
                    dve.wait_ge(wo_done, 2 * it + (b + 1))
                    x = xb(2 * it + b)
                    dve.tensor_tensor(x, x, P[7][:, S:2 * S].rearrange("p (u d) -> p u d", u=2), ALU.add)\
                       .then_inc(x2_done, 1)

            steps(dve, step)

            dve.wait_ge(x2_done, B)

            def ln3(b, first=False):
                stats(b, st3, mv3_ready, first)
                normalise(b, rs3_ready, t3_done, xn3_ready, first)

            def result(b):
                dve.wait_ge(yt3_done, b + 1)
                dve.tensor_tensor(xb(b), xb(b), P[6][:, 0:S].rearrange("p (u d) -> p u d", u=2), ALU.add)\
                   .then_inc(out_ready, 1)

            def ffn2(b, n):
                if n + 2 < B:
                    ln3(b + 2)
                if 0 <= n - 2 < B:
                    result(b - 2)

            ln3(0, True)
            ln3(1)
            ffn2(0, 0)
            ffn2(1, 1)
            with dve.Fori(2, B - 2) as b:
                ffn2(b, 2)
            for n in range(B - 2, B + 2):
                ffn2(n, n)

        @block.tensor
        def _(pe):
            pe.wait_ge(id_ready, 1)
            pe.wait_ge(wcon_in, 16)
            for c in range(C):
                ins = pe.transpose(P[7][:, c * 128:(c + 1) * 128], WDN[:, c, :], IDF[:, :])
            ins.then_inc(wc_t, 1)
            pe.wait_ge(rcol_in, 16 * 5)
            pe.wait_ge(row_folded, 1)
            pe.transpose(P[6][:, 0:C], ROW[:, (STAGES - 2) % 2, :], IDF[0:C, 0:C])
            pe.transpose(P[6][:, C:C + 8], RCOL[:, :], IDF[0:8, 0:8]).then_inc(col_t, 1)

            def t_x(b, ready, left, done, first=False):
                pe.wait_ge(ready, b + 1)
                if not first:
                    pe.wait_ge(left, b)
                for u in range(2):
                    ins = pe.transpose(P[0][:, u * 128:(u + 1) * 128], XN[:, u, :], IDF[:, :])
                ins.then_inc(done, 1)

            def up(b, c, ready, gelu_done, done, first=False):
                if c == 0:
                    pe.wait_ge(ready, b + 1)
                if not first:
                    pe.wait_ge(gelu_done[c], b)
                pe.matmul(P[1 + c][:, 0:S], WUP[:, STAGES % 2, c * 128:(c + 1) * 128],
                          XNT[:, one(b), :].rearrange("p o t -> p (o t)"), start=True, stop=True)\
                  .then_inc(done[c], 1)

            def down(b, gelu_done, ys_ready, done, first=False):
                if not first:
                    pe.wait_ge(ys_ready, b)
                for c in range(C):
                    pe.wait_ge(gelu_done[c], b + 1)
                    ins = pe.matmul(P[5][:, 0:S], WDN[:, c, :],
                                    HT[:, one(b), c, :].rearrange("p o t -> p (o t)"),
                                    start=c == 0, stop=c == C - 1)
                ins.then_inc(done, 1)

            def t_y(b, ys_ready, left, done, first=False):
                pe.wait_ge(ys_ready, b + 1)
                if not first:
                    pe.wait_ge(left, b)
                for u in range(2):
                    ins = pe.transpose(P[6][:, u * 128:(u + 1) * 128], YS[:, u * 128:(u + 1) * 128], IDF[:, :])
                ins.then_inc(done, 1)

            def up1(b, c, first=False):
                up(b, c, xnt1_ready, gelu1_done, up1_done, first)

            def t_x1(b, first=False):
                t_x(b, xn1_ready, xnt1_ready, t1_done, first)

            t_x1(0, True)
            pe.wait_ge(up_stage, STAGES)
            up1(0, 0, True)
            up1(0, 1, True)
            t_x1(1)
            up1(0, 2, True)
            up1(0, 3, True)
            with pe.Fori(1, B - 1) as b:
                up1(b, 0)
                up1(b, 1)
                t_x1(b + 1)
                up1(b, 2)
                up1(b, 3)
            for c in range(C):
                up1(B - 1, c)

            pe.wait_ge(dn_stage, STAGES)
            for c in range(C):
                ins = pe.transpose(P[7][:, c * 128:(c + 1) * 128],
                                   WDT[:, STAGES % 2, c * 128:(c + 1) * 128], IDF[:, :])
            ins.then_inc(wdn_t, 1)
            pe.wait_ge(wdn_ready, 1)

            def t_x2(b, first=False):
                t_x(b, xn2_ready, xn2t_ready, t2_done, first)

            def qkv(b, first=False):
                pe.wait_ge(xn2t_ready, b + 1)
                if not first:
                    pe.wait_ge(part1_done, b)
                for n, w in enumerate((WQP, WKP)):
                    ins = pe.matmul(P[7][:, n * S:(n + 1) * S], w[:, :], XN2T[:, :], start=True, stop=True)
                ins.then_inc(qk_done, 1)
                if not first:
                    pe.wait_ge(vb_ready, b)
                for j in range(J):
                    for par in range(2):
                        w = WVs[:, :].rearrange("k (f c n) -> k f c n", f=2, c=2)[:, :, par, :]
                        ins = pe.matmul(P[1][64 * par:64 * par + 64, 64 * j:64 * j + 64],
                                        XN2T[:, 64 * j:64 * j + 64], w, start=True, stop=True)
                ins.then_inc(v_done, 1)

            pe.wait_ge(wqk_ready, 2)
            down(0, gelu1_done, ys1_ready, down1_done, True)
            t_y(0, ys1_ready, x1_done, yt1_done, True)
            down(1, gelu1_done, ys1_ready, down1_done)
            t_x2(0, True)
            t_y(1, ys1_ready, x1_done, yt1_done)
            qkv(0, True)
            with pe.Fori(1, B - 1) as b:
                down(b + 1, gelu1_done, ys1_ready, down1_done)
                t_x2(b)
                t_y(b + 1, ys1_ready, x1_done, yt1_done)
                qkv(b)
            t_x2(B - 1)
            qkv(B - 1)

            pe.wait_ge(const, CONSTS)
            pe.wait_ge(msk_ready, 4)
            pe.wait_ge(idb_ready, 1)

            def mask(ps, m, cols, first):
                n = cols // 64
                return pe.matmul(ps, IDB[:, :], MSK[:, m, 0:n, :], start=first, stop=False, skip_group_check=True)

            def scores_max(g, k, t, it):
                u = g % 4
                ps = P[bank(g, k)]
                if k == 0:
                    pe.wait_ge(stack_in[u], (it + (g // 4 + 1)) * 80)
                if k >= 2:
                    pe.wait_ge(max_done[k - 2], t)
                elif g >= 1:
                    pe.wait_ge(max_done[k + 3], t - 1)
                if k < HP:
                    mask(ps[:, 192:320], 0, 128, True)
                    mask(ps[:, 448:512], 0, 64, False)
                    todo = [(j, k, at) for j, at in MAX_AT.items()]
                else:
                    mask(ps[:, :].rearrange("p (a w) -> p a w", w=128)[:, :, 64:128], 0, 256, True)
                    todo = [(1, hp, 128 * hp) for hp in range(HP)]
                for j, hp, at in todo:
                    for par in range(2):
                        h = head(par, hp)
                        ins = pe.matmul(ps[64 * par:64 * par + 64, at:at + 64 * (j + 1)],
                                        QS[:, u, h, 64 * j:64 * j + 64], KS[:, u, h, 0:64 * (j + 1)],
                                        start=False, stop=True, skip_group_check=True)
                ins.then_inc(s1_done[k], 1)

            def scores_exp(g, k, t, it):
                u = g % 4
                ps = P[2 + bank(g, k)]
                if k == 0:
                    pe.wait_ge(m_in[u], (it + (g // 4 + 1)) * 32)
                if k >= 2:
                    pe.wait_ge(exp_done[k - 2], t)
                elif g >= 1:
                    pe.wait_ge(exp_done[k + 3], t - 1)
                if k < HP:
                    mask(ps[:, 0:128], 1, 128, True)
                    mask(ps[:, 320:384], 1, 64, False)
                    todo = [(i, k, at) for i, at in EXP_AT.items()]
                else:
                    mask(ps[:, :].rearrange("p (a w) -> p a w", w=128)[:, :, 0:64], 1, 256, True)
                    todo = [(2, hp, 128 * hp) for hp in range(HP)]
                for i, hp, at in todo:
                    for par in range(2):
                        h = head(par, hp)
                        ins = pe.matmul(ps[64 * par:64 * par + 64, at:at + S - 64 * i],
                                        KS[:, u, h, 64 * i:64 * i + 64],
                                        QS[:, u, h, 64 * i:S],
                                        start=False, stop=True, skip_group_check=True)
                ins.then_inc(s2_done[k], 1)

            def pv(g, t, it):
                pe.wait_ge(exp_done[4], t)
                pe.wait_ge(v_in[g // 2 % 2], (it + (g // 4 + 1)) * 16)
                if g >= 1:
                    pe.wait_ge(ot_ready, t - 1)
                for i in range(J):
                    for hp in range(HP):
                        px = PX[:, g % 2, 4, 128 * hp:128 * hp + 128] if i == 2 else \
                            PX[:, g % 2, hp, EXP_AT[i]:EXP_AT[i] + S - 64 * i]
                        ins = pe.matmul(P[4][VW * hp:VW * (hp + 1), 64 * i:S],
                                        VS[:, g // 2 % 2, HP * (g % 2) + hp, i, :], px,
                                        start=i == 0, stop=i == J - 1)
                ins.then_inc(pv_done, 1)

            def step(s, t, it):
                def s1(k):
                    if 0 <= s + 2 < UNITS:
                        scores_max(s + 2, k, t + 3, it)

                def s2(k):
                    if 0 <= s < UNITS:
                        scores_exp(s, k, t + 1, it)

                s1(0)
                s2(0)
                s1(1)
                if 0 <= s + 1 < UNITS:
                    pe.wait_ge(mp_ready, t + 2)
                    if s + 1 >= 1:
                        pe.wait_ge(mts_ready, t + 1)
                    pe.transpose(P[5][:, 0:64].bitcast(BF16),
                                 MP[:, :, :].rearrange("p i n -> p (i n)"), IDB[:, :]).then_inc(mt_done, 1)
                b = (s - 3) // 2
                has_z = s % 2 and 0 <= b < B
                if has_z:
                    pe.wait_ge(z_ready, 2 * it + (b + 1))
                    if b >= 1:
                        pe.wait_ge(x2_done, 2 * it + b)
                    for u in range(2):
                        ins = pe.transpose(P[7][0:DH, u * 128:(u + 1) * 128], Z[:, u, :], IDF[:, :])
                    ins.then_inc(zt_done, 1)
                s2(1)
                if 0 <= s - 1 < UNITS:
                    pv(s - 1, t, it if (s - 1) % 4 != 3 or s < 0 else it)
                s1(2)
                s2(2)
                s1(3)
                if 0 <= s - 1 < UNITS:
                    pe.wait_ge(ot_ready, t)
                    if s - 1 >= 1:
                        pe.wait_ge(zh_ready, t - 1)
                    for u in range(2):
                        ins = pe.transpose(P[6][:, u * 128:(u + 1) * 128], OT[:, u * 128:(u + 1) * 128], IDF[:, :])
                    ins.then_inc(ott_done, 1)
                s2(3)
                s1(4)
                if has_z:
                    pe.wait_ge(zts_ready, 2 * it + (b + 1))
                    for u in range(2):
                        ins = pe.matmul(P[7][:, S + u * 128:S + (u + 1) * 128], ZT[:, u * 128:(u + 1) * 128],
                                        WOs[:, :], start=True, stop=True)
                    ins.then_inc(wo_done, 1)
                s2(4)

            steps(pe, step)

            def ffn2(b, n):
                def up3(c):
                    up(b, c, xnt3_ready, gelu3_done, up3_done, n == 0)

                if n < B:
                    up3(0)
                    up3(1)
                if n + 1 < B:
                    t_x(b + 1, xn3_ready, xnt3_ready, t3_done)
                if 0 <= n - 2 < B:
                    t_y(b - 2, ys3_ready, out_ready, yt3_done, n == 2)
                if n < B:
                    up3(2)
                    up3(3)
                if 0 <= n - 1 < B:
                    down(b - 1, gelu3_done, ys3_ready, down3_done, n == 1)

            t_x(0, xn3_ready, xnt3_ready, t3_done, True)
            ffn2(0, 0)
            ffn2(1, 1)
            ffn2(2, 2)
            with pe.Fori(3, B - 1) as b:
                ffn2(b, 3)
            for n in range(B - 1, B + 2):
                ffn2(n, n)


_INS = ["x", "WQ", "bQ", "WK", "bK", "WV", "bV", "WO", "bO"]
_FFN = ["W_exp", "b_exp", "up_weights", "up_bias", "down_weights", "W_con", "b_con", "down_bias"]


def kernel(**inputs):
    import numpy as np
    import concourse.bacc as bacc
    from concourse import mybir as mb
    from concourse.bass_utils import run_bass_kernel_spmd as run

    nc = bacc.Bacc("TRN2", target_bir_lowering=False, num_devices=1)
    arrays, args = {}, []
    for name in ["L0_attn_" + n for n in _INS] + ["L0_ffn_" + n for n in _FFN]:
        a = np.ascontiguousarray(inputs[name])
        arrays[name] = a
        args.append(nc.dram_tensor(name, a.shape, mb.dt.from_np(a.dtype), kind="ExternalInput").ap())
    out = nc.dram_tensor("out", (B, S, D), F32, kind="ExternalOutput").ap()
    build(nc, *args, out)
    return run(nc, [arrays], core_ids=[0]).results[0]["out"]
```

```python
import concourse.bass as bass
from concourse import mybir
from contextlib import ExitStack

F32 = mybir.dt.float32
BF16 = mybir.dt.bfloat16
ALU = mybir.AluOpType
ACT = mybir.ActivationFunctionType
AX = mybir.AxisListType

B, S, D, H = 8, 256, 128, 16
DH = D // H
HID = 4 * D
C = HID // D
STAGES = HID.bit_length() - 1
EPS = 1e-5
SCALE = float(DH) ** -0.5
MASKED = -1e30
HH = H // 2
HP = HH // 2
J = S // 64
UNITS = 2 * B
PARTS = 3
ROWS = PARTS * PARTS * DH
VW = 32

MAX_AT = {3: 0, 0: 256, 2: 320}
EXP_AT = {3: 0, 0: 64, 1: 320}


def build(nc, x, WQ, bQ, WK, bK, WV, bV, WO, bO, W_exp, b_exp, up_w, up_b, down_w, W_con, b_con, down_b, out):
    ctx = ExitStack()
    with ctx:
        def sb(name, shape, dt=F32):
            return ctx.enter_context(nc.sbuf_tensor(name, shape, dt))

        def sem(name):
            return ctx.enter_context(nc.semaphore(name))

        X = sb("X", [128, B, 2, D])
        HT = sb("HT", [128, B, C, S])
        XNT = sb("XNT", [128, B, S])
        XN = sb("XN", [128, 2, 2, D])
        XN2T = sb("XN2T", [128, S])
        YS = sb("YS", [128, S])
        ST1 = sb("ST1", [128, 2 * B, 6])
        ST = sb("ST", [128, 2, 6])
        VE = sb("VE", [128, 2])
        MV1 = sb("MV1", [128, B, 2, 2])
        RS1 = sb("RS1", [128, B, 2])
        MV = sb("MV", [128, 2, 2])
        RS = sb("RS", [128, 2])
        POW = sb("POW", [128, B * 2])
        WUP = sb("WUP", [128, 2, HID])
        WDT = sb("WDT", [128, 2, HID])
        TM = sb("TM", [128, 2, HID])
        WDN = sb("WDN", [128, C, D])
        BW = sb("BW", [128, STAGES, 1024])
        WQs = sb("WQs", [128, D])
        WKs = sb("WKs", [128, D])
        WVs = sb("WVs", [128, D])
        WQP = sb("WQP", [128, D])
        WKP = sb("WKP", [128, D])
        WOs = sb("WOs", [DH + 1, D])
        BV = sb("BV", [128, D])
        BVP = sb("BVP", [128, D // 2])
        ROW = sb("ROW", [C, 2, D])
        RTM = sb("RTM", [C, 2, D])
        RW = sb("RW", [C, STAGES - 2, 256])
        RCOL = sb("RCOL", [8, D])
        COL = sb("COL", [128, 12])
        CW = sb("CW", [128, 2, 2, 4])
        CT = sb("CT", [128, 3, C])
        BUP = sb("BUP", [128, C])
        BQS = sb("BQS", [128, 1])
        BY = sb("BY", [128, 2])
        IDF = sb("IDF", [128, 128])
        IDB = sb("IDB", [128, 128], BF16)
        TRI = sb("TRI", [128, 2, 128])
        MSK = sb("MSK", [128, 2, 4, 64], BF16)
        QKF = sb("QKF", [128, 2, S])
        RES = sb("RES", [128, 2, S])
        PR = sb("PR", [128, 2, 2, PARTS, S], BF16)
        QS = sb("QS", [128, 4, HH, S], BF16)
        KS = sb("KS", [128, 4, HH, S], BF16)
        VA = sb("VA", [128, B, 2 * D])
        OWN = sb("OWN", [128, 2])
        VS = sb("VS", [128, 2, H // 2, J, VW])
        PX = HT[:, 0:5, :, :].rearrange("p b c t -> p (b c t)")\
            .rearrange("p (g k n) -> p g k n", g=2, k=5)
        ONES = sb("ONES", [128, 2], BF16)
        PM = sb("PM", [128, 2, 5, 8])
        NM = sb("NM", [128, HP, J])
        NR = sb("NR", [128, HP * J])
        MP = sb("MP", [128, 8, HP * J], BF16)
        ZC = sb("ZC", [128, HP * J])
        EPSC = sb("EPSC", [128, 2])
        HOLD = sb("HOLD", [128, 1])
        HOLDP = sb("HOLDP", [128, 1])
        MT = sb("MT", [PARTS * HP * J, 128], BF16)
        OT = sb("OT", [128, S])
        RD = sb("RD", [128, 2 * HH])
        ZH = sb("ZH", [128, 2, DH, H])
        Z = sb("Z", [128, 2, DH])
        ZT = sb("ZT", [DH + 1, S])
        P = [ctx.enter_context(nc.psum_tensor(f"P{i}", [128, 512], F32)) for i in range(8)]
        scr_q = nc.dram_tensor("scr_q", [B, ROWS + PARTS, H, S], BF16).ap()
        scr_k = nc.dram_tensor("scr_k", [B, PARTS * DH, H, S], BF16).ap()

        x_in = [sem(f"x_in{i}") for i in range(2)]
        w_in = sem("w_in")
        wup_in = sem("wup_in")
        wcon_in = sem("wcon_in")
        rcol_in = sem("rcol_in")
        cw_in = sem("cw_in")
        own_ready = sem("own_ready")
        vs_ready = sem("vs_ready")
        wqk_ready = sem("wqk_ready")
        idb_ready = sem("idb_ready")
        dn_stage = sem("dn_stage")
        col_t = sem("col_t")
        xc1_ready = sem("xc1_ready")
        rs1_ready = sem("rs1_ready")
        ve2_ready = sem("ve2_ready")
        ve3_ready = sem("ve3_ready")
        upw_in = [sem(f"upw_in{s}") for s in range(STAGES)]
        dnw_in = [sem(f"dnw_in{s}") for s in range(STAGES)]
        row_in = sem("row_in")
        const = sem("const")
        id_ready = sem("id_ready")
        tri_ready = sem("tri_ready")
        msk_ready = sem("msk_ready")
        dve_chain = sem("dve_chain")
        pool_chain = sem("pool_chain")
        ln1_stats = sem("ln1_stats")
        up_stage = sem("up_stage")
        wc_t = sem("wc_t")
        wdt_ready = sem("wdt_ready")
        wdn_t = sem("wdn_t")
        wdn_ready = sem("wdn_ready")
        row_folded = sem("row_folded")
        col_ready = sem("col_ready")
        bias_ready = sem("bias_ready")
        xn1_ready = sem("xn1_ready")
        t1_done = sem("t1_done")
        xnt1_ready = sem("xnt1_ready")
        up1_done = [sem(f"up1_done{c}") for c in range(C)]
        gelu1_done = [sem(f"gelu1_done{c}") for c in range(C)]
        down1_done = sem("down1_done")
        ys1_ready = sem("ys1_ready")
        yt1_done = sem("yt1_done")
        x1_done = sem("x1_done")
        st2 = sem("st2")
        mv2_ready = sem("mv2_ready")
        rs2_ready = sem("rs2_ready")
        xn2_ready = sem("xn2_ready")
        t2_done = sem("t2_done")
        xn2t_ready = sem("xn2t_ready")
        qk_done = sem("qk_done")
        v_done = sem("v_done")
        qkf_ready = sem("qkf_ready")
        part1_done = sem("part1_done")
        res_ready = sem("res_ready")
        part2_done = sem("part2_done")
        part3_done = sem("part3_done")
        vb_ready = sem("vb_ready")
        scr_out = [sem(f"scr_out{p}") for p in range(2)]
        zeros_out = sem("zeros_out")
        fills = sem("fills")
        stack_in = [sem(f"stack_in{u}") for u in range(4)]
        s1_done = [sem(f"s1_done{k}") for k in range(5)]
        max_done = [sem(f"max_done{k}") for k in range(5)]
        nm_ready = sem("nm_ready")
        mp1 = sem("mp1")
        mp2 = sem("mp2")
        mp3 = sem("mp3")
        mp_ready = sem("mp_ready")
        mt_done = sem("mt_done")
        mts_ready = sem("mts_ready")
        m_in = [sem(f"m_in{u}") for u in range(4)]
        s2_done = [sem(f"s2_done{k}") for k in range(5)]
        exp_done = [sem(f"exp_done{k}") for k in range(5)]
        pv_done = sem("pv_done")
        ot_ready = sem("ot_ready")
        ott_done = sem("ott_done")
        rd_ready = sem("rd_ready")
        zh_ready = sem("zh_ready")
        z_ready = sem("z_ready")
        zt_done = sem("zt_done")
        zts_ready = sem("zts_ready")
        wo_done = sem("wo_done")
        x2_done = sem("x2_done")
        st3 = sem("st3")
        mv3_ready = sem("mv3_ready")
        rs3_ready = sem("rs3_ready")
        xn3_ready = sem("xn3_ready")
        t3_done = sem("t3_done")
        xnt3_ready = sem("xnt3_ready")
        up3_done = [sem(f"up3_done{c}") for c in range(C)]
        gelu3_done = [sem(f"gelu3_done{c}") for c in range(C)]
        down3_done = sem("down3_done")
        ys3_ready = sem("ys3_ready")
        yt3_done = sem("yt3_done")
        out_ready = sem("out_ready")
        out_sent = sem("out_sent")

        CONSTS = 6
        up_flat = up_w.rearrange("s k a c -> s (k a c)")
        down_flat = down_w.rearrange("s k a c -> s (k a c)")

        FIRST, LAST = -2, UNITS + 2
        LOOP_FROM, ROUNDS = 5, 2

        def steps(eng, step):
            for s in range(FIRST, LOOP_FROM):
                step(s, s, 0)
            with eng.Fori(0, ROUNDS) as it:
                for s in range(LOOP_FROM, LOOP_FROM + 4):
                    step(s, it * 4 + s, it)
            for s in range(LOOP_FROM + 4 * ROUNDS, LAST + 1):
                step(s, s, 0)

        def batches(eng, step):
            step(0, 0)
            step(1, 1)
            with eng.Fori(0, B // 2 - 2) as it:
                step(it * 2 + 2, 2)
                step(it * 2 + 3, 3)
            step(B - 2, B - 2)
            step(B - 1, B - 1)

        def one(b):
            return bass.ds(b, 1)

        def xb(b):
            return X[:, one(b), :, :].rearrange("p o u d -> p (o u) d")

        def bank(g, k):
            return (5 * g + k) % 2

        def head(par, hp):
            return HP * par + hp

        block = ctx.enter_context(nc.Block())

        @block.sync
        def _(sp):
            def load_x(n):
                half = slice(n * B // 2, (n + 1) * B // 2)
                sp.dma_start(X[:, half, :, :].rearrange("p b u d -> p (b u) d"),
                             x[half].rearrange("b (u p) d -> p (b u) d", p=128)).then_inc(x_in[n], 16)

            load_x(0)
            sp.dma_start(WUP[:, 0, :], W_exp).then_inc(wup_in, 16)
            for s in range(STAGES):
                sp.dma_start(BW[:, s, :], up_flat[s].partition_broadcast(128)).then_inc(upw_in[s], 16)
                if s == 3:
                    load_x(1)
            for n in range(STAGES):
                sp.wait_ge(up_stage, n + 1)
                sp.dma_start(BW[:, n, :], down_flat[STAGES - 1 - n].partition_broadcast(128))\
                  .then_inc(dnw_in[n], 16)
                if n == 3:
                    for w, of in ((WQs[:, :], WQ), (WKs[:, :], WK), (WVs[:, :], WV), (WOs[0:DH, :], WO),
                                  (WOs[DH:DH + 1, :], bO.rearrange("(o n) -> o n", o=1)),
                                  (BV[:, :], bV.partition_broadcast(128))):
                        sp.dma_start(w, of).then_inc(w_in, 16)
            sp.wait_ge(fills, 2)
            sp.dma_start(scr_q[:, ROWS:ROWS + PARTS, :, :].rearrange("b r h t -> r b (h t)"),
                         QS[ROWS:ROWS + PARTS, 0:2, :, :].rearrange("r u h t -> r (u h t)").unsqueeze(1)
                         .to_broadcast([PARTS, B, H * S])).then_inc(zeros_out, 16)

            def load_unit(u, b, half):
                heads = slice(half * HH, (half + 1) * HH)
                sp.dma_start(QS[0:ROWS + PARTS, u, :, :].rearrange("p h t -> p (h t)"),
                             scr_q[one(b), :, heads, :].rearrange("o r h t -> (o r) (h t)"))\
                  .then_inc(stack_in[u], 16)
                src = scr_k[one(b), :, heads, :].rearrange("o r h t -> o r (h t)")
                sp.dma_start(KS[0:ROWS, u, :, :].rearrange("p h t -> p (h t)"),
                             src.to_broadcast([PARTS, PARTS * DH, HH * S])).then_inc(stack_in[u], 16)

            def parts_out(b, n):
                sp.wait_ge(part3_done, b + 1)
                if n == 2:
                    sp.wait_ge(scr_out[0], 64)
                    sp.wait_ge(zeros_out, 16)
                if n == B - 2:
                    sp.wait_ge(scr_out[1], 64)
                for j in range(PARTS):
                    dst = scr_q[one(b), 0:ROWS, :, :].rearrange("o (i j d) h t -> j (o d h) i t", i=PARTS, j=PARTS)[j]
                    sp.dma_start(dst, PR[:, n % 2, 0, :, :]).then_inc(scr_out[n % 2], 16)
                sp.dma_start(scr_k[one(b)].rearrange("o (j d) h t -> (o d h) j t", j=PARTS),
                             PR[:, n % 2, 1, :, :]).then_inc(scr_out[n % 2], 16)
                if n == B - 2:
                    for g in range(4):
                        load_unit(g, g // 2, g % 2)

            batches(sp, parts_out)
            for p in range(2):
                sp.wait_ge(scr_out[p], 64 * B // 2)

            def step(s, t, it):
                g = s + 3
                if 4 <= g < UNITS:
                    sp.wait_ge(s2_done[4], t)
                    load_unit(g % 4, 2 * it + g // 2, g % 2)
                g = s + 1
                if 0 <= g < UNITS:
                    sp.wait_ge(mts_ready, t + 2)
                    for par in range(2):
                        sp.dma_start(QS[ROWS:ROWS + PARTS, g % 4, HP * par:HP * (par + 1), :]
                                     .rearrange("i h t -> i (h t)"),
                                     MT[:, 64 * par:64 * par + 64]).then_inc(m_in[g % 4], 16)

            steps(sp, step)

            with sp.Fori(0, B) as b:
                sp.wait_ge(out_ready, b + 1)
                sp.dma_start(out[one(b)].rearrange("o (u p) d -> p (o u) d", p=128), xb(b))\
                  .then_inc(out_sent, 16)
            sp.wait_ge(out_sent, 16 * B)

        @block.gpsimd
        def _(pool):
            chain = [0]

            def link(ins):
                chain[0] += 1
                ins.then_inc(pool_chain, 1)
                pool.wait_ge(pool_chain, chain[0])

            link(pool.memset(IDF[:, :], 0.0))
            pool.affine_select(out=IDF[:, :], in_=IDF[:, :], compare_op=ALU.not_equal, fill=1.0, base=0,
                               pattern=[[-1, 128]], channel_multiplier=1).then_inc(id_ready, 1)
            pool.memset(ONES[:, :], 1.0).then_inc(const, 1)
            pool.memset(ZC[:, :], 0.0).then_inc(const, 1)
            pool.memset(MP[:, :, :], 0.0).then_inc(const, 1)
            pool.memset(ZT[:, :], float(H)).then_inc(const, 1)
            pool.memset(POW[:, :], -0.5).then_inc(const, 1)
            pool.memset(EPSC[:, :], EPS).then_inc(const, 1)

            link(pool.memset(TRI[:, :, :], 0.0))
            pool.affine_select(out=TRI[:, 0, :], in_=TRI[:, 0, :], compare_op=ALU.is_ge, fill=MASKED,
                               base=0, pattern=[[-1, 128]], channel_multiplier=1).then_inc(tri_ready, 1)
            pool.affine_select(out=TRI[:, 1, :], in_=TRI[:, 1, :], compare_op=ALU.is_ge, fill=MASKED,
                               base=0, pattern=[[1, 128]], channel_multiplier=-1).then_inc(tri_ready, 1)

            pool.wait_ge(row_in, 32)
            for s in range(STAGES - 2):
                w = 2 ** s
                y = ROW[:, s % 2, :].rearrange("p (n a w) -> p n a w", a=2, w=w)
                W = RW[:, s, :].rearrange("p (n w a c) -> p n w a c", w=w, a=2, c=2)
                for i in range(2):
                    ins = pool.tensor_tensor(RTM[:, i, :].rearrange("p (n a w) -> p n a w", a=2, w=w),
                                             W[:, :, :, :, i].rearrange("p n w a -> p n a w"),
                                             y[:, :, i:i + 1, :].to_broadcast([C, D // (2 * w), 2, w]), ALU.mult)
                link(ins)
                ins = pool.tensor_tensor(ROW[:, (s + 1) % 2, :], RTM[:, 0, :], RTM[:, 1, :], ALU.add)
                if s < STAGES - 3:
                    link(ins)
            ins.then_inc(row_folded, 1)

            def rstd1(n):
                half = slice(n * B // 2, (n + 1) * B // 2)
                pool.wait_ge(ln1_stats, n + 1)
                link(pool.tensor_scalar(MV1[:, half, :, 1], MV1[:, half, :, 1], EPS, None, ALU.add))
                link(pool.tensor_tensor(RS1[:, half, :].rearrange("p b u -> p (b u)"),
                                        MV1[:, half, :, 1].rearrange("p b u -> p (b u)"), POW[:, 0:B], ALU.pow))

            def xn1(b, n):
                if n >= 2:
                    pool.wait_ge(t1_done, b - 1)
                xn = XN[:, n % 2, :, :]
                pool.tensor_tensor(xn, xb(b), MV1[:, one(b), :, 0:1].rearrange("p o u c -> p (o u) c")
                                   .to_broadcast([128, 2, D]), ALU.subtract).then_inc(xc1_ready, 1)
                pool.wait_ge(xc1_ready, b + 1)
                pool.tensor_tensor(xn, xn, RS1[:, one(b), :].rearrange("p o u -> p (o u)").unsqueeze(2)
                                   .to_broadcast([128, 2, D]), ALU.mult).then_inc(xn1_ready, 1)

            rstd1(0)

            pool.wait_ge(col_ready, 1)
            pool.wait_ge(cw_in, 32)
            for i in range(2):
                ins = pool.tensor_tensor(
                    CT[:, i, :].rearrange("p (n a) -> p n a", a=2), CW[:, 0, :, :]
                    .rearrange("p n (a c) -> p n a c", c=2)[:, :, :, i],
                    COL[:, 0:C].rearrange("p (n c) -> p n c", c=2)[:, :, i:i + 1].to_broadcast([128, 2, 2]), ALU.mult)
            link(ins)
            link(pool.tensor_tensor(CT[:, 2, :], CT[:, 0, :], CT[:, 1, :], ALU.add))
            for i in range(2):
                ins = pool.tensor_tensor(
                    CT[:, i, :].rearrange("p (a n) -> p n a", a=2), CW[:, 1, :, :]
                    .rearrange("p n (a c) -> p n a c", c=2)[:, :, :, i],
                    CT[:, 2, :].rearrange("p (c n) -> p n c", c=2)[:, :, i:i + 1].to_broadcast([128, 2, 2]), ALU.mult)
            link(ins)
            link(pool.tensor_tensor(CT[:, 2, :], CT[:, 0, :], CT[:, 1, :], ALU.add))
            pool.tensor_tensor(BUP[:, :], CT[:, 2, :], COL[:, 4:8], ALU.add).then_inc(bias_ready, 1)
            pool.tensor_scalar(BQS[:, :], COL[:, 8:9], SCALE, None, ALU.mult).then_inc(bias_ready, 1)
            link(pool.tensor_tensor(BY[:, 0:1], COL[:, 10:11], COL[:, 11:12], ALU.add))
            pool.tensor_scalar(BY[:, 1:2], BY[:, 0:1], 0.5, None, ALU.mult).then_inc(bias_ready, 1)

            xn1(0, 0)
            xn1(1, 1)
            with pool.Fori(1, B // 4) as it:
                xn1(it * 2, 2)
                xn1(it * 2 + 1, 3)
            rstd1(1)
            with pool.Fori(B // 4, B // 2) as it:
                xn1(it * 2, 2)
                xn1(it * 2 + 1, 3)

            link(pool.memset(VS[:, :, :, :, :], 0.0))
            for par in range(2):
                at = VW // 2 * par + DH
                ins = pool.memset(VS[64 * par:64 * par + 64, :, :, :, at:at + 1]
                                  .rearrange("p b a j w -> p (b a j) w"), 1.0)
            link(ins)

            def rstd2(b):
                pool.wait_ge(mv2_ready, b + 1)
                pool.tensor_tensor(VE[:, :], MV[:, :, 1], EPSC[:, :], ALU.add).then_inc(ve2_ready, 1)
                pool.wait_ge(ve2_ready, b + 1)
                pool.tensor_tensor(RS[:, :], VE[:, :], POW[:, 0:2], ALU.pow).then_inc(rs2_ready, 1)

            def residue(b, n):
                if n < B - 1:
                    rstd2(b + 1)
                pool.wait_ge(part1_done, b + 1)
                if n >= 1:
                    pool.wait_ge(part3_done, b)
                pool.tensor_tensor(RES[:, :, :], QKF[:, :, :], PR[:, n % 2, :, 0, :], ALU.subtract)\
                    .then_inc(res_ready, 1)

            rstd2(0)
            batches(pool, residue)

            def step(s, t, it):
                b = s // 2
                if s % 2 == 0 and 0 <= b < B:
                    if b >= 2:
                        pool.wait_ge(pv_done, t - 2)
                    pool.tensor_tensor(HOLDP[:, :], ZC[:, 0:1], ZC[:, 0:1], ALU.add)
                    n = H // 2 * J
                    pool.tensor_tensor(VS[:, b % 2, :, :, :].rearrange("p a j (c w) -> p (a j) c w", c=2)[:, :, :, 0:DH],
                                       VA[:, one(2 * it + b), :].rearrange("p o (n d) -> p (o n) d", d=DH)
                                       .unsqueeze(2).to_broadcast([128, n, 2, DH]),
                                       OWN[:, :].unsqueeze(1).unsqueeze(3).to_broadcast([128, n, 2, DH]),
                                       ALU.mult).then_inc(vs_ready, 1)
                g = s + 2
                if 0 <= g < UNITS:
                    nm = NM[:, :, :].rearrange("p a j -> p (a j)")
                    pool.wait_ge(nm_ready, t + 3)
                    if g >= 1:
                        pool.wait_ge(mt_done, t + 2)
                    pool.tensor_tensor(MP[:, 0, :], nm, ZC[:, :], ALU.add).then_inc(mp1, 1)
                    pool.wait_ge(mp1, t + 3)
                    pool.tensor_tensor(NR[:, :], nm, MP[:, 0, :], ALU.subtract).then_inc(mp2, 1)
                    pool.wait_ge(mp2, t + 3)
                    pool.tensor_tensor(MP[:, 1, :], NR[:, :], ZC[:, :], ALU.add).then_inc(mp3, 1)
                    pool.wait_ge(mp3, t + 3)
                    pool.tensor_tensor(MP[:, 2, :], NR[:, :], MP[:, 1, :], ALU.subtract).then_inc(mp_ready, 1)

            pool.wait_ge(vb_ready, B)
            pool.wait_ge(own_ready, 2)
            steps(pool, step)

            with pool.Fori(0, B) as b:
                pool.wait_ge(mv3_ready, b + 1)
                pool.tensor_tensor(VE[:, :], MV[:, :, 1], EPSC[:, :], ALU.add).then_inc(ve3_ready, 1)
                pool.wait_ge(ve3_ready, b + 1)
                pool.tensor_tensor(RS[:, :], VE[:, :], POW[:, 0:2], ALU.pow).then_inc(rs3_ready, 1)

        @block.scalar
        def _(act):
            act.dma_start(ROW[:, 0, :], b_exp.rearrange("(c n) -> c n", c=C)).then_inc(row_in, 16)
            act.dma_start(RW[:, :, :], up_flat[0:STAGES - 2].rearrange("s (c n) -> c s n", c=C))\
                .then_inc(row_in, 16)
            act.dma_start(WDN[:, :, :], W_con.rearrange("(c p) e -> p c e", p=128)).then_inc(wcon_in, 16)
            act.dma_start(RCOL[0:C, :], up_b.rearrange("(c n) -> c n", c=C)).then_inc(rcol_in, 16)
            for n, v in ((4, bQ), (5, bK)):
                act.dma_start(RCOL[n:n + 1, :].rearrange("o (d h) -> o d h", h=H),
                              v.rearrange("(o h d) -> o d h", o=1, h=H),
                               allow_slow_non_contiguous=True).then_inc(rcol_in, 16)
            for n, v in ((6, b_con), (7, down_b)):
                act.dma_start(RCOL[n:n + 1, :], v.rearrange("(o n) -> o n", o=1)).then_inc(rcol_in, 16)
            for m in range(2):
                act.dma_start(CW[:, m, :, :], up_w[STAGES - 2 + m].rearrange("(n p) a c -> p n (a c)", p=128))\
                    .then_inc(cw_in, 16)

            act.wait_ge(const, CONSTS)
            for dst, of in ((KS, ONES[:, :].bitcast(F32)), (QS, ZC[:, 0:1])):
                dst = dst[:, :, :, :].rearrange("p u h t -> p (u h t)").bitcast(F32)
                act.activation(dst, of.to_broadcast([128, 4 * HH * S // 2]), ACT.Copy).then_inc(fills, 1)

            act.wait_ge(wc_t, 1)
            act.activation(WDT[:, 0, :], P[7][:, :], ACT.Copy).then_inc(wdt_ready, 1)
            act.wait_ge(col_t, 1)
            act.activation(COL[:, 0:12], P[6][:, 0:12], ACT.Copy).then_inc(col_ready, 1)

            act.activation(IDB[:, :], IDF[:, :], ACT.Copy).then_inc(idb_ready, 1)
            act.wait_ge(tri_ready, 2)
            for par in range(2):
                rows = slice(64 * par, 64 * par + 64)
                for m in range(2):
                    act.activation(MSK[rows, m, :, :], TRI[rows, m, 64 * par:64 * par + 64].unsqueeze(1)
                                   .to_broadcast([64, 4, 64]), ACT.Copy).then_inc(msk_ready, 1)

            def gelu(b, c, up_done, gelu_done):
                act.wait_ge(up_done[c], b + 1)
                act.activation(HT[:, one(b), c, :].rearrange("p o t -> p (o t)"), P[1 + c][:, 0:S],
                               ACT.Gelu, bias=BUP[:, c:c + 1]).then_inc(gelu_done[c], 1)

            def xnt(b, t_done, ready):
                act.wait_ge(t_done, b + 1)
                act.activation(XNT[:, one(b), :].rearrange("p o t -> p (o t)"), P[0][:, 0:S], ACT.Copy)\
                   .then_inc(ready, 1)

            def ys(b, down_done, ready):
                act.wait_ge(down_done, b + 1)
                act.activation(YS[:, :], P[5][:, 0:S], ACT.Identity, bias=BY[:, 1:2], scale=0.5)\
                   .then_inc(ready, 1)

            xnt(0, t1_done, xnt1_ready)
            act.wait_ge(bias_ready, 3)

            xnt(1, t1_done, xnt1_ready)

            def gelus1(b, n):
                gelu(b, 0, up1_done, gelu1_done)
                gelu(b, 1, up1_done, gelu1_done)
                if n + 2 < B:
                    xnt(b + 2, t1_done, xnt1_ready)
                gelu(b, 2, up1_done, gelu1_done)
                gelu(b, 3, up1_done, gelu1_done)

            gelus1(0, 0)
            with act.Fori(1, B - 2) as b:
                gelus1(b, 1)
            gelus1(B - 2, B - 2)
            gelus1(B - 1, B - 1)

            act.wait_ge(w_in, 16 * 6)
            for dst, w in ((WQP, WQs), (WKP, WKs)):
                act.activation(dst[:, :].rearrange("k (d h) -> k d h", h=H),
                               w[:, :].rearrange("k (h d) -> k d h", h=H), ACT.Copy).then_inc(wqk_ready, 1)

            def ys1(b, first=False):
                if not first:
                    act.wait_ge(yt1_done, b)
                ys(b, down1_done, ys1_ready)

            def xn2t(b, first=False):
                if not first:
                    act.wait_ge(v_done, b)
                act.wait_ge(t2_done, b + 1)
                act.activation(XN2T[:, :], P[0][:, 0:S], ACT.Copy).then_inc(xn2t_ready, 1)

            def qk(b, n):
                if n >= 1:
                    act.wait_ge(res_ready, b)
                if n >= 2:
                    act.wait_ge(scr_out[n % 2], (b - n % 2) * 32)
                act.wait_ge(qk_done, b + 1)
                for m, (bias, scale) in enumerate(((BQS[:, :], SCALE), (COL[:, 9:10], 1.0))):
                    for dst in (QKF[:, m, :], PR[:, n % 2, m, 0, :]):
                        ins = act.activation(dst, P[7][:, m * S:(m + 1) * S], ACT.Identity,
                                             bias=bias, scale=scale)
                ins.then_inc(part1_done, 1)

            def half2(b, n):
                if n < B - 1:
                    ys1(b + 1)
                xn2t(b, n == 0)
                qk(b, n)

            ys1(0, True)
            batches(act, half2)

            def exps(g, k, t):
                act.wait_ge(s2_done[k], t)
                act.activation(PX[:, g % 2, k, :], P[2 + bank(g, k)][:, :], ACT.Exp).then_inc(exp_done[k], 1)

            def step(s, t, it):
                def ex(k):
                    if 0 <= s < UNITS:
                        exps(s, k, t + 1)

                if 0 <= s < UNITS and s >= 2:
                    act.wait_ge(pv_done, t - 1)
                ex(0)
                g = s + 1
                if 0 <= g < UNITS:
                    act.wait_ge(mt_done, t + 2)
                    if g >= 1:
                        act.wait_ge(m_in[s % 4], (it + (s // 4 + 1)) * 32)
                    act.activation(MT[:, :], P[5][0:PARTS * HP * J, 0:64].bitcast(BF16), ACT.Copy)\
                       .then_inc(mts_ready, 1)
                ex(1)
                ex(2)
                ex(3)
                b = (s - 3) // 2
                if s % 2 and 0 <= b < B:
                    act.wait_ge(zt_done, 2 * it + (b + 1))
                    if b >= 1:
                        act.wait_ge(wo_done, 2 * it + b)
                    act.activation(ZT[0:DH, :], P[7][0:DH, 0:S], ACT.Copy).then_inc(zts_ready, 1)
                if 0 <= s - 1 < UNITS:
                    act.wait_ge(pv_done, t)
                    if s >= 2:
                        act.wait_ge(ott_done, t - 1)
                    act.activation(OT[:, :], P[4][:, 0:S], ACT.Copy).then_inc(ot_ready, 1)
                ex(4)

            steps(act, step)

            def ys3(b, first=False):
                if not first:
                    act.wait_ge(yt3_done, b)
                ys(b, down3_done, ys3_ready)

            def ffn2(b, n):
                if n < B:
                    gelu(b, 0, up3_done, gelu3_done)
                    gelu(b, 1, up3_done, gelu3_done)
                if n + 1 < B:
                    xnt(b + 1, t3_done, xnt3_ready)
                if n < B:
                    gelu(b, 2, up3_done, gelu3_done)
                    gelu(b, 3, up3_done, gelu3_done)
                if 0 <= n - 1 < B:
                    ys3(b - 1, n == 1)

            xnt(0, t3_done, xnt3_ready)
            ffn2(0, 0)
            ffn2(1, 1)
            with act.Fori(2, B - 1) as b:
                ffn2(b, 2)
            for n in range(B - 1, B + 1):
                ffn2(n, n)

        @block.vector
        def _(dve):
            chain = [0]

            def link(ins):
                chain[0] += 1
                ins.then_inc(dve_chain, 1)
                dve.wait_ge(dve_chain, chain[0])

            def stats1(half):
                dve.wait_ge(x_in[half], 16)
                tiles = range(half * B, half * B + B)
                for n in tiles:
                    ins = dve.bn_stats(ST1[:, n, :], X[:, n // 2, n % 2, :])
                link(ins)
                for n in tiles:
                    ins = dve.bn_aggr(MV1[:, n // 2, n % 2, :], ST1[:, n, :])
                ins.then_inc(ln1_stats, 1)

            link(dve.memset(OWN[:, :], 0.0))
            for par in range(2):
                dve.memset(OWN[64 * par:64 * par + 64, par:par + 1], 1.0).then_inc(own_ready, 1)
            stats1(0)

            def stage(W, y, o, w, transposed, done):
                yv = y.rearrange("p (n a w) -> p n a w", a=2, w=w)
                Wv = W.rearrange("p (n w a c) -> p n w a c", w=w, a=2, c=2)
                for i in range(2):
                    wv = Wv[:, :, :, :, i].rearrange("p n w a -> p n a w") if not transposed else \
                        Wv[:, :, :, i, :].rearrange("p n w a -> p n a w")
                    ins = dve.tensor_tensor(TM[:, i, :].rearrange("p (n a w) -> p n a w", a=2, w=w), wv,
                                            yv[:, :, i:i + 1, :].to_broadcast([128, HID // (2 * w), 2, w]), ALU.mult)
                link(ins)
                ins = dve.tensor_tensor(o, TM[:, 0, :], TM[:, 1, :], ALU.add)
                done(ins)

            dve.wait_ge(wup_in, 16)
            for s in range(STAGES):
                dve.wait_ge(upw_in[s], 16)

                def done(ins):
                    ins.then_inc(up_stage, 1)
                    dve.wait_ge(up_stage, s + 1)
                stage(BW[:, s, :], WUP[:, s % 2, :], WUP[:, (s + 1) % 2, :], 2 ** s, False, done)
            stats1(1)
            dve.wait_ge(wdt_ready, 1)
            for n in range(STAGES):
                dve.wait_ge(dnw_in[n], 16)

                def done(ins):
                    ins.then_inc(dn_stage, 1)
                    dve.wait_ge(dn_stage, n + 1)
                stage(BW[:, n, :], WDT[:, n % 2, :], WDT[:, (n + 1) % 2, :], 2 ** (STAGES - 1 - n), True, done)
            dve.wait_ge(wdn_t, 1)
            dve.tensor_copy(WDN[:, :, :].rearrange("p c e -> p (c e)"), P[7][:, :]).then_inc(wdn_ready, 1)

            dve.wait_ge(w_in, 16 * 6)

            def stats(b, st_done, mv_done, first):
                for u in range(2):
                    ins = dve.bn_stats(ST[:, u, :], X[:, one(b), u, :].rearrange("p o d -> p (o d)"))
                ins.then_inc(st_done, 1)
                dve.wait_ge(st_done, b + 1)
                dve.memset(HOLD[:, :], 0.0)
                for u in range(2):
                    ins = dve.bn_aggr(MV[:, u, :], ST[:, u, :])
                ins.then_inc(mv_done, 1)

            def normalise(b, rs_ready, left, ready, first):
                if not first:
                    dve.wait_ge(left, b)
                dve.wait_ge(rs_ready, b + 1)
                for u in range(2):
                    ins = dve.tensor_scalar(XN[:, 0, u, :], X[:, one(b), u, :].rearrange("p o d -> p (o d)"),
                                            MV[:, u, 0:1], RS[:, u:u + 1], ALU.subtract, ALU.mult)
                ins.then_inc(ready, 1)

            def x1_stats(b, first=False):
                dve.wait_ge(yt1_done, b + 1)
                dve.tensor_tensor(xb(b), xb(b), P[6][:, 0:S].rearrange("p (u d) -> p u d", u=2), ALU.add)\
                   .then_inc(x1_done, 1)
                dve.wait_ge(x1_done, b + 1)
                dve.memset(HOLD[:, :], 0.0)
                stats(b, st2, mv2_ready, first)

            def v_blocks(b):
                dve.wait_ge(v_done, b + 1)
                dve.tensor_tensor(VA[:, one(b), :].rearrange("p o (a j d) -> p (o a) j d", j=J, d=DH),
                                  P[1][:, 0:S].rearrange("p (j a d) -> p a j d", j=J, d=DH),
                                  BVP[:, :].rearrange("p (a d) -> p a d", d=DH).unsqueeze(2)
                                  .to_broadcast([128, H // 2, J, DH]), ALU.add).then_inc(vb_ready, 1)

            def parts(b, n):
                dve.wait_ge(res_ready, b + 1)
                dve.tensor_copy(PR[:, n % 2, :, 1, :], RES[:, :, :]).then_inc(part2_done, 1)
                dve.wait_ge(part2_done, b + 1)
                dve.tensor_tensor(PR[:, n % 2, :, 2, :], RES[:, :, :], PR[:, n % 2, :, 1, :], ALU.subtract)\
                   .then_inc(part3_done, 1)

            for par in range(2):
                rows = slice(64 * par, 64 * par + 64)
                ins = dve.tensor_copy(
                    BVP[rows, :].rearrange("p (f n) -> p f n", f=2),
                    BV[rows, :].rearrange("p (f c n) -> p f c n", f=2, c=2)[:, :, par, :])
            link(ins)


            def half2(b, n):
                if n < B - 1:
                    x1_stats(b + 1)
                v_blocks(b)
                if n < B - 1:
                    normalise(b + 1, rs2_ready, t2_done, xn2_ready, False)
                parts(b, n)

            x1_stats(0, True)
            normalise(0, rs2_ready, t2_done, xn2_ready, True)
            batches(dve, half2)

            def maxima(g, k, t):
                dve.wait_ge(s1_done[k], t)
                dve.tensor_reduce(PM[:, g % 2, k, :], P[bank(g, k)][:, :].rearrange("p (n w) -> p n w", w=64),
                                  AX.X, ALU.max).then_inc(max_done[k], 1)

            def step(s, t, it):
                def mx(k):
                    if 0 <= s + 2 < UNITS:
                        maxima(s + 2, k, t + 3)

                mx(0)
                b = (s - 4) // 2
                if s % 2 == 0 and 0 <= b < B:
                    dve.wait_ge(wo_done, 2 * it + (b + 1))
                    x = xb(2 * it + b)
                    dve.tensor_tensor(x, x, P[7][:, S:2 * S].rearrange("p (u d) -> p u d", u=2), ALU.add)\
                       .then_inc(x2_done, 1)
                mx(1)
                mx(2)
                g = s - 2
                if 0 <= g < UNITS:
                    dve.wait_ge(ott_done, t - 1)
                    o = P[6][:, 0:2 * 128].rearrange("p (n w) -> p n w", w=VW // 2)
                    dve.reciprocal(RD[:, :], o[:, :, DH]).then_inc(rd_ready, 1)
                    dve.wait_ge(rd_ready, t - 1)
                    at = HH * (g % 2)
                    dve.tensor_tensor(ZH[:, :, :, at:at + HH].rearrange("p u d h -> p u h d"),
                                      P[6][:, 0:2 * 128].rearrange("p (u h w) -> p u h w", u=2, w=VW // 2)[:, :, :, 0:DH],
                                      RD[:, :].rearrange("p (u h) -> p u h", u=2).unsqueeze(3)
                                      .to_broadcast([128, 2, HH, DH]), ALU.mult).then_inc(zh_ready, 1)
                    if g % 2:
                        dve.wait_ge(zh_ready, t - 1)
                        if g >= 2:
                            dve.wait_ge(zt_done, 2 * it + g // 2)
                        dve.tensor_reduce(Z[:, :, :].rearrange("p u d -> p (u d)"),
                                          ZH[:, :, :, :].rearrange("p u d h -> p (u d) h"),
                                          AX.X, ALU.add).then_inc(z_ready, 1)
                mx(3)
                mx(4)
                g = s + 2
                if 0 <= g < UNITS:
                    if g >= 1:
                        dve.wait_ge(mp2, t + 2)
                    dve.wait_ge(max_done[4], t + 3)
                    pm = PM[:, g % 2, :, :]
                    for j, of in ((3, pm[:, 0:HP, 0:4]), (0, pm[:, 0:HP, 4:5]), (2, pm[:, 0:HP, 5:8]),
                                  (1, pm[:, HP, :].rearrange("p (a j) -> p a j", j=2))):
                        ins = dve.tensor_reduce(NM[:, :, j], of, AX.X, ALU.max, negate=True)
                    ins.then_inc(nm_ready, 1)

            steps(dve, step)

            dve.wait_ge(x2_done, B)

            def ln3(b, first=False):
                stats(b, st3, mv3_ready, first)
                normalise(b, rs3_ready, t3_done, xn3_ready, first)

            def result(b):
                dve.wait_ge(yt3_done, b + 1)
                dve.tensor_tensor(xb(b), xb(b), P[6][:, 0:S].rearrange("p (u d) -> p u d", u=2), ALU.add)\
                   .then_inc(out_ready, 1)

            def ffn2(b, n):
                if n + 2 < B:
                    ln3(b + 2)
                if 0 <= n - 2 < B:
                    result(b - 2)

            ln3(0, True)
            ln3(1)
            ffn2(0, 0)
            ffn2(1, 1)
            with dve.Fori(2, B - 2) as b:
                ffn2(b, 2)
            for n in range(B - 2, B + 2):
                ffn2(n, n)

        @block.tensor
        def _(pe):
            pe.wait_ge(id_ready, 1)
            pe.wait_ge(wcon_in, 16)
            for c in range(C):
                ins = pe.transpose(P[7][:, c * 128:(c + 1) * 128], WDN[:, c, :], IDF[:, :])
            ins.then_inc(wc_t, 1)
            pe.wait_ge(rcol_in, 16 * 5)
            pe.wait_ge(row_folded, 1)
            pe.transpose(P[6][:, 0:C], ROW[:, (STAGES - 2) % 2, :], IDF[0:C, 0:C])
            pe.transpose(P[6][:, C:C + 8], RCOL[:, :], IDF[0:8, 0:8]).then_inc(col_t, 1)

            def t_x(b, ready, left, done, first=False, slot=0):
                pe.wait_ge(ready, b + 1)
                if not first:
                    pe.wait_ge(left, b)
                for u in range(2):
                    ins = pe.transpose(P[0][:, u * 128:(u + 1) * 128], XN[:, slot, u, :], IDF[:, :])
                ins.then_inc(done, 1)

            def up(b, c, ready, gelu_done, done, first=False):
                if c == 0:
                    pe.wait_ge(ready, b + 1)
                if not first:
                    pe.wait_ge(gelu_done[c], b)
                pe.matmul(P[1 + c][:, 0:S], WUP[:, STAGES % 2, c * 128:(c + 1) * 128],
                          XNT[:, one(b), :].rearrange("p o t -> p (o t)"), start=True, stop=True)\
                  .then_inc(done[c], 1)

            def down(b, gelu_done, ys_ready, done, first=False):
                if not first:
                    pe.wait_ge(ys_ready, b)
                for c in range(C):
                    pe.wait_ge(gelu_done[c], b + 1)
                    ins = pe.matmul(P[5][:, 0:S], WDN[:, c, :],
                                    HT[:, one(b), c, :].rearrange("p o t -> p (o t)"),
                                    start=c == 0, stop=c == C - 1)
                ins.then_inc(done, 1)

            def t_y(b, ys_ready, left, done, first=False):
                pe.wait_ge(ys_ready, b + 1)
                if not first:
                    pe.wait_ge(left, b)
                for u in range(2):
                    ins = pe.transpose(P[6][:, u * 128:(u + 1) * 128], YS[:, u * 128:(u + 1) * 128], IDF[:, :])
                ins.then_inc(done, 1)

            def up1(b, c, first=False):
                up(b, c, xnt1_ready, gelu1_done, up1_done, first)

            def t_x1(b, n):
                t_x(b, xn1_ready, xnt1_ready, t1_done, n == 0, n % 2)

            def half1(b, n):
                up1(b, 0, n == 0)
                up1(b, 1, n == 0)
                if n + 2 < B:
                    t_x1(b + 2, n + 2)
                up1(b, 2, n == 0)
                up1(b, 3, n == 0)

            t_x1(0, 0)
            t_x1(1, 1)
            pe.wait_ge(up_stage, STAGES)
            batches(pe, half1)

            pe.wait_ge(dn_stage, STAGES)
            for c in range(C):
                ins = pe.transpose(P[7][:, c * 128:(c + 1) * 128],
                                   WDT[:, STAGES % 2, c * 128:(c + 1) * 128], IDF[:, :])
            ins.then_inc(wdn_t, 1)
            pe.wait_ge(wdn_ready, 1)

            def t_x2(b, first=False):
                t_x(b, xn2_ready, xn2t_ready, t2_done, first)

            def qkv(b, first=False):
                pe.wait_ge(xn2t_ready, b + 1)
                if not first:
                    pe.wait_ge(part1_done, b)
                for n, w in enumerate((WQP, WKP)):
                    ins = pe.matmul(P[7][:, n * S:(n + 1) * S], w[:, :], XN2T[:, :], start=True, stop=True)
                ins.then_inc(qk_done, 1)
                if not first:
                    pe.wait_ge(vb_ready, b)
                for j in range(J):
                    for par in range(2):
                        w = WVs[:, :].rearrange("k (f c n) -> k f c n", f=2, c=2)[:, :, par, :]
                        ins = pe.matmul(P[1][64 * par:64 * par + 64, 64 * j:64 * j + 64],
                                        XN2T[:, 64 * j:64 * j + 64], w, start=True, stop=True)
                ins.then_inc(v_done, 1)

            pe.wait_ge(wqk_ready, 2)
            down(0, gelu1_done, ys1_ready, down1_done, True)
            t_y(0, ys1_ready, x1_done, yt1_done, True)
            down(1, gelu1_done, ys1_ready, down1_done)
            t_x2(0, True)
            t_y(1, ys1_ready, x1_done, yt1_done)
            qkv(0, True)
            with pe.Fori(1, B - 1) as b:
                down(b + 1, gelu1_done, ys1_ready, down1_done)
                t_x2(b)
                t_y(b + 1, ys1_ready, x1_done, yt1_done)
                qkv(b)
            t_x2(B - 1)
            qkv(B - 1)

            pe.wait_ge(vb_ready, B)
            pe.wait_ge(fills, 2)
            pe.wait_ge(msk_ready, 4)
            pe.wait_ge(idb_ready, 1)

            def mask(ps, m, cols, first):
                n = cols // 64
                return pe.matmul(ps, IDB[:, :], MSK[:, m, 0:n, :], start=first, stop=False, skip_group_check=True)

            def scores_max(g, k, t, it):
                u = g % 4
                ps = P[bank(g, k)]
                if k == 0:
                    pe.wait_ge(stack_in[u], (it + (g // 4 + 1)) * 32)
                if k >= 2:
                    pe.wait_ge(max_done[k - 2], t)
                elif g >= 1:
                    pe.wait_ge(max_done[k + 3], t - 1)
                if k < HP:
                    mask(ps[:, 192:320], 0, 128, True)
                    mask(ps[:, 448:512], 0, 64, False)
                    todo = [(j, k, at) for j, at in MAX_AT.items()]
                else:
                    mask(ps[:, :].rearrange("p (a w) -> p a w", w=128)[:, :, 64:128], 0, 256, True)
                    todo = [(1, hp, 128 * hp) for hp in range(HP)]
                for j, hp, at in todo:
                    for par in range(2):
                        h = head(par, hp)
                        ins = pe.matmul(ps[64 * par:64 * par + 64, at:at + 64 * (j + 1)],
                                        QS[:, u, h, 64 * j:64 * j + 64], KS[:, u, h, 0:64 * (j + 1)],
                                        start=False, stop=True, skip_group_check=True)
                ins.then_inc(s1_done[k], 1)

            def scores_exp(g, k, t, it):
                u = g % 4
                ps = P[2 + bank(g, k)]
                if k == 0:
                    pe.wait_ge(m_in[u], (it + (g // 4 + 1)) * 32)
                if k >= 2:
                    pe.wait_ge(exp_done[k - 2], t)
                elif g >= 1:
                    pe.wait_ge(exp_done[k + 3], t - 1)
                if k < HP:
                    mask(ps[:, 0:128], 1, 128, True)
                    mask(ps[:, 320:384], 1, 64, False)
                    todo = [(i, k, at) for i, at in EXP_AT.items()]
                else:
                    mask(ps[:, :].rearrange("p (a w) -> p a w", w=128)[:, :, 0:64], 1, 256, True)
                    todo = [(2, hp, 128 * hp) for hp in range(HP)]
                for i, hp, at in todo:
                    for par in range(2):
                        h = head(par, hp)
                        ins = pe.matmul(ps[64 * par:64 * par + 64, at:at + S - 64 * i],
                                        KS[:, u, h, 64 * i:64 * i + 64],
                                        QS[:, u, h, 64 * i:S],
                                        start=False, stop=True, skip_group_check=True)
                ins.then_inc(s2_done[k], 1)

            def pv(g, t, it):
                pe.wait_ge(exp_done[4], t)
                if g % 2 == 0:
                    pe.wait_ge(vs_ready, 2 * it + (g // 2 + 1))
                if g >= 1:
                    pe.wait_ge(ot_ready, t - 1)
                for i in range(J):
                    for hp in range(HP):
                        px = PX[:, g % 2, 4, 128 * hp:128 * hp + 128] if i == 2 else \
                            PX[:, g % 2, hp, EXP_AT[i]:EXP_AT[i] + S - 64 * i]
                        ins = pe.matmul(P[4][VW * hp:VW * (hp + 1), 64 * i:S],
                                        VS[:, g // 2 % 2, HP * (g % 2) + hp, i, :], px,
                                        start=i == 0, stop=i == J - 1)
                ins.then_inc(pv_done, 1)

            def step(s, t, it):
                def s1(k):
                    if 0 <= s + 2 < UNITS:
                        scores_max(s + 2, k, t + 3, it)

                def s2(k):
                    if 0 <= s < UNITS:
                        scores_exp(s, k, t + 1, it)

                s1(0)
                s2(0)
                s1(1)
                if 0 <= s + 1 < UNITS:
                    pe.wait_ge(mp_ready, t + 2)
                    if s + 1 >= 1:
                        pe.wait_ge(mts_ready, t + 1)
                    pe.transpose(P[5][:, 0:64].bitcast(BF16),
                                 MP[:, :, :].rearrange("p i n -> p (i n)"), IDB[:, :]).then_inc(mt_done, 1)
                s2(1)
                if 0 <= s - 2 < UNITS:
                    pe.wait_ge(ot_ready, t - 1)
                    if s - 2 >= 1:
                        pe.wait_ge(zh_ready, t - 2)
                    for u in range(2):
                        ins = pe.transpose(P[6][:, u * 128:(u + 1) * 128], OT[:, u * 128:(u + 1) * 128], IDF[:, :])
                    ins.then_inc(ott_done, 1)
                s1(2)
                s2(2)
                s1(3)
                s2(3)
                s1(4)
                b = (s - 3) // 2
                has_z = s % 2 and 0 <= b < B
                if has_z:
                    pe.wait_ge(z_ready, 2 * it + (b + 1))
                    for u in range(2):
                        ins = pe.transpose(P[7][0:DH, u * 128:(u + 1) * 128], Z[:, u, :], IDF[:, :])
                    ins.then_inc(zt_done, 1)
                if 0 <= s - 1 < UNITS:
                    pv(s - 1, t, it)
                s2(4)
                if has_z:
                    pe.wait_ge(zts_ready, 2 * it + (b + 1))
                    if b >= 1:
                        pe.wait_ge(x2_done, 2 * it + b)
                    for u in range(2):
                        ins = pe.matmul(P[7][:, S + u * 128:S + (u + 1) * 128], ZT[:, u * 128:(u + 1) * 128],
                                        WOs[:, :], start=True, stop=True)
                    ins.then_inc(wo_done, 1)

            steps(pe, step)

            def ffn2(b, n):
                def up3(c):
                    up(b, c, xnt3_ready, gelu3_done, up3_done, n == 0)

                if n < B:
                    up3(0)
                    up3(1)
                if n + 1 < B:
                    t_x(b + 1, xn3_ready, xnt3_ready, t3_done)
                if 0 <= n - 2 < B:
                    t_y(b - 2, ys3_ready, out_ready, yt3_done, n == 2)
                if n < B:
                    up3(2)
                    up3(3)
                if 0 <= n - 1 < B:
                    down(b - 1, gelu3_done, ys3_ready, down3_done, n == 1)

            t_x(0, xn3_ready, xnt3_ready, t3_done, True)
            ffn2(0, 0)
            ffn2(1, 1)
            ffn2(2, 2)
            with pe.Fori(3, B - 1) as b:
                ffn2(b, 3)
            for n in range(B - 1, B + 2):
                ffn2(n, n)


_INS = ["x", "WQ", "bQ", "WK", "bK", "WV", "bV", "WO", "bO"]
_FFN = ["W_exp", "b_exp", "up_weights", "up_bias", "down_weights", "W_con", "b_con", "down_bias"]


def kernel(**inputs):
    import numpy as np
    import concourse.bacc as bacc
    from concourse import mybir as mb
    from concourse.bass_utils import run_bass_kernel_spmd as run

    nc = bacc.Bacc("TRN2", target_bir_lowering=False, num_devices=1)
    arrays, args = {}, []
    for name in ["L0_attn_" + n for n in _INS] + ["L0_ffn_" + n for n in _FFN]:
        a = np.ascontiguousarray(inputs[name])
        arrays[name] = a
        args.append(nc.dram_tensor(name, a.shape, mb.dt.from_np(a.dtype), kind="ExternalInput").ap())
    out = nc.dram_tensor("out", (B, S, D), F32, kind="ExternalOutput").ap()
    build(nc, *args, out)
    return run(nc, [arrays], core_ids=[0]).results[0]["out"]
```

```python
import concourse.bass as bass
from concourse import mybir
from contextlib import ExitStack

F32 = mybir.dt.float32
BF16 = mybir.dt.bfloat16
ALU = mybir.AluOpType
ACT = mybir.ActivationFunctionType
AX = mybir.AxisListType

B, S, D, H = 8, 256, 128, 16
DH = D // H
HID = 4 * D
C = HID // D
STAGES = HID.bit_length() - 1
EPS = 1e-5
SCALE = float(DH) ** -0.5
MASKED = -1e30
HH = H // 2
HP = HH // 2
J = S // 64
UNITS = 2 * B
PARTS = 3
ROWS = PARTS * PARTS * DH
VW = 32

MAX_AT = {3: 0, 0: 256, 2: 320}
EXP_AT = {3: 0, 0: 64, 1: 320}


def build(nc, x, WQ, bQ, WK, bK, WV, bV, WO, bO, W_exp, b_exp, up_w, up_b, down_w, W_con, b_con, down_b, out):
    ctx = ExitStack()
    with ctx:
        def sb(name, shape, dt=F32):
            return ctx.enter_context(nc.sbuf_tensor(name, shape, dt))

        def sem(name):
            return ctx.enter_context(nc.semaphore(name))

        X = sb("X", [128, B, 2, D])
        HT = sb("HT", [128, B, C, S])
        XNT = sb("XNT", [128, B, S])
        XN = sb("XN", [128, 2, 2, D])
        XN2T = sb("XN2T", [128, S])
        YS = sb("YS", [128, S])
        SUM1 = sb("SUM1", [128, 2, 2 * B])
        ST = sb("ST", [128, 2, 6])
        VE = sb("VE", [128, 2])
        MV1 = sb("MV1", [128, 2, B, 2])
        RS1 = sb("RS1", [128, B, 2])
        MV = sb("MV", [128, 2, 2])
        RS = sb("RS", [128, 2])
        POW = sb("POW", [128, B * 2])
        WUP = sb("WUP", [128, 2, HID])
        WDT = sb("WDT", [128, 2, HID])
        TM = sb("TM", [128, 2, HID])
        TMP = sb("TMP", [128, 2, 128])
        WDN = sb("WDN", [128, C, D])
        BW = sb("BW", [128, STAGES, 1024])
        PR = BW[:, :, :].rearrange("p s n -> p (s n)").bitcast(BF16)[:, 0:B * 2 * PARTS * S]\
            .rearrange("p (b q i t) -> p b q i t", b=B, q=2, i=PARTS)
        WQs = sb("WQs", [128, D])
        WKs = sb("WKs", [128, D])
        WVs = sb("WVs", [128, D])
        WQP = sb("WQP", [128, D])
        WKP = sb("WKP", [128, D])
        WOs = sb("WOs", [DH + 1, D])
        BV = sb("BV", [128, D])
        BVP = sb("BVP", [128, D // 2])
        ROW = sb("ROW", [C, 2, D])
        RTM = sb("RTM", [C, 2, D])
        RW = sb("RW", [C, STAGES - 2, 256])
        RCOL = sb("RCOL", [8, D])
        COL = sb("COL", [128, 12])
        CW = sb("CW", [128, 2, 2, 4])
        CT = sb("CT", [128, 3, C])
        BUP = sb("BUP", [128, C])
        BQS = sb("BQS", [128, 1])
        BY = sb("BY", [128, 2])
        IDF = sb("IDF", [128, 128])
        IDB = sb("IDB", [128, 128], BF16)
        WARM = sb("WARM", [128, 1])
        TRI = sb("TRI", [128, 2, 128])
        MSK = sb("MSK", [128, 2, 4, 64], BF16)
        QKF = sb("QKF", [128, 2, 2, S])
        RES = sb("RES", [128, 2, 2, S])
        QS = sb("QS", [128, 4, HH, S], BF16)
        KS = sb("KS", [128, 4, HH, S], BF16)
        VA = sb("VA", [128, B, 2 * D])
        OWN = sb("OWN", [128, 2])
        VS = sb("VS", [128, 2, H // 2, J, VW])
        PX = HT[:, 0:5, :, :].rearrange("p b c t -> p (b c t)")\
            .rearrange("p (g k n) -> p g k n", g=2, k=5)
        PM = sb("PM", [128, 2, 5, 8])
        NM = sb("NM", [128, HP, J])
        NR = sb("NR", [128, HP * J])
        MP = sb("MP", [128, 8, HP * J], BF16)
        ZC = sb("ZC", [128, HP * J])
        EPSC = sb("EPSC", [128, 2])
        HOLD = sb("HOLD", [128, 1])
        HOLDP = sb("HOLDP", [128, 1])
        MT = sb("MT", [PARTS * HP * J, 128], BF16)
        OT = sb("OT", [128, S])
        RD = sb("RD", [128, 2 * HH])
        ZH = sb("ZH", [128, 2, DH, H])
        Z = sb("Z", [128, 2, DH])
        ZT = sb("ZT", [DH + 1, S])
        P = [ctx.enter_context(nc.psum_tensor(f"P{i}", [128, 512], F32)) for i in range(8)]
        scr_q = nc.dram_tensor("scr_q", [B, ROWS + PARTS, H, S], BF16).ap()
        scr_k = nc.dram_tensor("scr_k", [B, PARTS * DH, H, S], BF16).ap()

        x_in = [sem(f"x_in{i}") for i in range(2)]
        w_in = sem("w_in")
        wup_in = sem("wup_in")
        wcon_in = sem("wcon_in")
        rcol_in = sem("rcol_in")
        cw_in = sem("cw_in")
        own_ready = sem("own_ready")
        vs_ready = sem("vs_ready")
        wqk_ready = sem("wqk_ready")
        idb_ready = sem("idb_ready")
        dn_stage = sem("dn_stage")
        dn_chunk = sem("dn_chunk")
        col_t = sem("col_t")
        xc1_ready = sem("xc1_ready")
        ve2_ready = sem("ve2_ready")
        ve3_ready = sem("ve3_ready")
        upw_in = [sem(f"upw_in{s}") for s in range(STAGES)]
        dnw_in = [sem(f"dnw_in{s}") for s in range(STAGES)]
        row_in = sem("row_in")
        const = sem("const")
        id_ready = sem("id_ready")
        tri_ready = sem("tri_ready")
        msk_ready = sem("msk_ready")
        dve_chain = sem("dve_chain")
        pool_chain = sem("pool_chain")
        ln1_sum = sem("ln1_sum")
        ln1_mean = sem("ln1_mean")
        ln1_stats = sem("ln1_stats")
        up_stage = sem("up_stage")
        wc_t = sem("wc_t")
        wdt_ready = sem("wdt_ready")
        wdn_t = sem("wdn_t")
        wdn_ready = sem("wdn_ready")
        row_folded = sem("row_folded")
        col_ready = sem("col_ready")
        bias_ready = sem("bias_ready")
        xn1_ready = sem("xn1_ready")
        t1_done = sem("t1_done")
        xnt1_ready = sem("xnt1_ready")
        up1_done = [sem(f"up1_done{c}") for c in range(C)]
        gelu1_done = [sem(f"gelu1_done{c}") for c in range(C)]
        down1_done = sem("down1_done")
        ys1_ready = sem("ys1_ready")
        yt1_done = sem("yt1_done")
        x1_done = sem("x1_done")
        st2 = sem("st2")
        mv2_ready = sem("mv2_ready")
        rs2_ready = sem("rs2_ready")
        xn2_ready = sem("xn2_ready")
        t2_done = sem("t2_done")
        xn2t_ready = sem("xn2t_ready")
        qk_done = sem("qk_done")
        v_done = sem("v_done")
        part1_done = sem("part1_done")
        res_ready = sem("res_ready")
        part2_done = sem("part2_done")
        part3_done = sem("part3_done")
        vb_ready = sem("vb_ready")
        scr_out = [sem(f"scr_out{p}") for p in range(2)]
        scr_last = sem("scr_last")
        zeros_out = sem("zeros_out")
        fills = sem("fills")
        stack_in = [sem(f"stack_in{u}") for u in range(4)]
        s1_done = [sem(f"s1_done{k}") for k in range(5)]
        max_done = [sem(f"max_done{k}") for k in range(5)]
        nm_ready = sem("nm_ready")
        mp1 = sem("mp1")
        mp2 = sem("mp2")
        mp3 = sem("mp3")
        mp_ready = sem("mp_ready")
        mt_done = sem("mt_done")
        mts_ready = sem("mts_ready")
        m_in = [sem(f"m_in{u}") for u in range(4)]
        s2_done = [sem(f"s2_done{k}") for k in range(5)]
        exp_done = [sem(f"exp_done{k}") for k in range(5)]
        pv_done = sem("pv_done")
        ot_ready = sem("ot_ready")
        ott_done = sem("ott_done")
        rd_ready = sem("rd_ready")
        zh_ready = sem("zh_ready")
        z_ready = sem("z_ready")
        zt_done = sem("zt_done")
        zts_ready = sem("zts_ready")
        wo_done = sem("wo_done")
        x2_done = sem("x2_done")
        st3 = sem("st3")
        mv3_ready = sem("mv3_ready")
        rs3_ready = sem("rs3_ready")
        xn3_ready = sem("xn3_ready")
        t3_done = sem("t3_done")
        xnt3_ready = sem("xnt3_ready")
        up3_done = [sem(f"up3_done{c}") for c in range(C)]
        gelu3_done = [sem(f"gelu3_done{c}") for c in range(C)]
        down3_done = sem("down3_done")
        ys3_ready = sem("ys3_ready")
        yt3_done = sem("yt3_done")
        out_ready = sem("out_ready")
        out_sent = sem("out_sent")

        CONSTS = 5
        up_flat = up_w.rearrange("s k a c -> s (k a c)")
        down_flat = down_w.rearrange("s k a c -> s (k a c)")

        SHARED = 5
        LN1 = (0, B // 4, B // 2, B)

        FIRST, LAST = 0, UNITS + 2
        LOOP_FROM, ROUNDS = 5, 2

        def steps(eng, step):
            for s in range(FIRST, LOOP_FROM):
                step(s, s, 0)
            with eng.Fori(0, ROUNDS) as it:
                for s in range(LOOP_FROM, LOOP_FROM + 4):
                    step(s, it * 4 + s, it)
            for s in range(LOOP_FROM + 4 * ROUNDS, LAST + 1):
                step(s, s, 0)

        def batches(eng, step, last=None):
            step(0, 0)
            step(1, 1)
            with eng.Fori(0, B // 2 - 2) as it:
                step(it * 2 + 2, 2)
                step(it * 2 + 3, 3)
            step(B - 2, B - 2)
            if last:
                last()
            else:
                step(B - 1, B - 1)

        def one(b):
            return bass.ds(b, 1)

        def xb(b):
            return X[:, one(b), :, :].rearrange("p o u d -> p (o u) d")

        def part(b, i):
            return PR[:, one(b), :, i, :].rearrange("p o q t -> p (o q) t")

        def max_in(eng, g, t):
            eng.wait_ge(mts_ready, t + 1)
            for par in range(2):
                eng.dma_start(QS[ROWS:ROWS + PARTS, g % 4, HP * par:HP * (par + 1), :]
                              .rearrange("i h t -> i (h t)"),
                              MT[:, 64 * par:64 * par + 64]).then_inc(m_in[g % 4], 16)

        def bank(g, k):
            return (5 * g + k) % 2

        def max_bank(g, k):
            return bank(g, k) + (2 if g < 2 else 0)

        def head(par, hp):
            return HP * par + hp


        def k_ones(eng, slots):
            eng.memset(KS[:, slots, :, :].rearrange("p u h t -> p (u h t)").bitcast(F32),
                       1.0 + 0x3F80 / 2 ** 23).then_inc(fills, 1)

        block = ctx.enter_context(nc.Block())

        @block.sync
        def _(sp):
            def load_x(n):
                half = slice(n * B // 2, (n + 1) * B // 2)
                sp.dma_start(X[:, half, :, :].rearrange("p b u d -> p (b u) d"),
                             x[half].rearrange("b (u p) d -> p (b u) d", p=128)).then_inc(x_in[n], 16)

            sp.dma_start(WUP[:, 0, :], W_exp).then_inc(wup_in, 16)
            for s in range(STAGES):
                sp.dma_start(BW[:, s, :], up_flat[s].partition_broadcast(128)).then_inc(upw_in[s], 16)
                if s in (3, 5):
                    load_x(s // 5)
            for n in range(STAGES):
                sp.wait_ge(up_stage, n + 1)
                sp.dma_start(BW[:, n, :], down_flat[STAGES - 1 - n].partition_broadcast(128))\
                  .then_inc(dnw_in[n], 16)
                if n == 3:
                    for w, of in ((WQs[:, :], WQ), (WKs[:, :], WK), (WVs[:, :], WV), (WOs[0:DH, :], WO),
                                  (WOs[DH:DH + 1, :], bO.rearrange("(o n) -> o n", o=1)),
                                  (BV[:, :], bV.partition_broadcast(128))):
                        sp.dma_start(w, of).then_inc(w_in, 16)
            sp.wait_ge(fills, 4)
            sp.dma_start(scr_q[:, ROWS:ROWS + PARTS, :, :].rearrange("b r h t -> r b (h t)"),
                         QS[ROWS:ROWS + PARTS, 0:2, :, :].rearrange("r u h t -> r (u h t)").unsqueeze(1)
                         .to_broadcast([PARTS, B, H * S])).then_inc(zeros_out, 16)

            def load_unit(u, b, half):
                heads = slice(half * HH, (half + 1) * HH)
                sp.dma_start(QS[0:ROWS + PARTS, u, :, :].rearrange("p h t -> p (h t)"),
                             scr_q[one(b), :, heads, :].rearrange("o r h t -> (o r) (h t)"))\
                  .then_inc(stack_in[u], 16)
                src = scr_k[one(b), :, heads, :].rearrange("o r h t -> o r (h t)")
                sp.dma_start(KS[0:ROWS, u, :, :].rearrange("p h t -> p (h t)"),
                             src.to_broadcast([PARTS, PARTS * DH, HH * S])).then_inc(stack_in[u], 16)

            def parts_out(b, done):
                sp.wait_ge(part3_done, b + 1)
                for j in range(PARTS):
                    dst = scr_q[one(b), 0:ROWS, :, :].rearrange("o (i j d) h t -> j (o d h) i t", i=PARTS, j=PARTS)[j]
                    sp.dma_start(dst, PR[:, one(b), 0, :, :].rearrange("p o i t -> p (o i) t")).then_inc(done, 16)
                sp.dma_start(scr_k[one(b)].rearrange("o (j d) h t -> (o d h) j t", j=PARTS),
                             PR[:, one(b), 1, :, :].rearrange("p o i t -> p (o i) t")).then_inc(done, 16)

            for b in range(2):
                parts_out(b, scr_out[b])
            sp.wait_ge(zeros_out, 16)
            for g in range(4):
                sp.wait_ge(scr_out[g // 2], 64)
                load_unit(g, g // 2, g % 2)
            with sp.Fori(2, B - 3) as b:
                parts_out(b, scr_out[0])

            def step(s, t, it):
                if s == 1:
                    sp.wait_ge(scr_out[0], 64 * (B - 4))
                if s == 3:
                    sp.wait_ge(scr_last, 64 * 3)
                g = s + 3
                if 4 <= g < UNITS:
                    sp.wait_ge(s2_done[4], t)
                    load_unit(g % 4, 2 * it + g // 2, g % 2)
                if s + 1 < UNITS:
                    max_in(sp, s + 1, t + 1)
                if s == 0:
                    parts_out(B - 3, scr_last)
                if s < 2:
                    parts_out(B - 2 + s, scr_last)

            steps(sp, step)

            with sp.Fori(0, B) as b:
                sp.wait_ge(out_ready, b + 1)
                sp.dma_start(out[one(b)].rearrange("o (u p) d -> p (o u) d", p=128), xb(b))\
                  .then_inc(out_sent, 16)
            sp.wait_ge(out_sent, 16 * B)

        @block.gpsimd
        def _(pool):
            chain = [0]

            def link(ins):
                chain[0] += 1
                ins.then_inc(pool_chain, 1)
                pool.wait_ge(pool_chain, chain[0])

            link(pool.memset(IDF[:, :], 0.0))
            pool.affine_select(out=IDF[:, :], in_=IDF[:, :], compare_op=ALU.not_equal, fill=1.0, base=0,
                               pattern=[[-1, 128]], channel_multiplier=1).then_inc(id_ready, 1)
            pool.memset(ZC[:, :], 0.0).then_inc(const, 1)
            pool.memset(MP[:, :, :], 0.0).then_inc(const, 1)
            pool.memset(ZT[:, :], float(H)).then_inc(const, 1)
            pool.memset(POW[:, :], -0.5).then_inc(const, 1)
            pool.memset(EPSC[:, :], EPS).then_inc(const, 1)

            link(pool.memset(TRI[:, :, :], 0.0))
            pool.affine_select(out=TRI[:, 0, :], in_=TRI[:, 0, :], compare_op=ALU.is_ge, fill=MASKED,
                               base=0, pattern=[[-1, 128]], channel_multiplier=1).then_inc(tri_ready, 1)
            pool.affine_select(out=TRI[:, 1, :], in_=TRI[:, 1, :], compare_op=ALU.is_ge, fill=MASKED,
                               base=0, pattern=[[1, 128]], channel_multiplier=-1).then_inc(tri_ready, 1)

            def mean1(n):
                half = slice(n * B // 2, (n + 1) * B // 2)
                pool.wait_ge(ln1_sum, n + 1)
                pool.tensor_scalar(MV1[:, 0, half, :].rearrange("p b u -> p (b u)"), SUM1[:, 0, n * B:(n + 1) * B],
                                   -1.0 / D, None, ALU.mult).then_inc(ln1_mean, 1)

            pool.wait_ge(row_in, 32)
            for s in range(STAGES - 2):
                if s == STAGES - 3:
                    mean1(0)
                w = 2 ** s
                y = ROW[:, s % 2, :].rearrange("p (n a w) -> p n a w", a=2, w=w)
                W = RW[:, s, :].rearrange("p (n w a c) -> p n w a c", w=w, a=2, c=2)
                for i in range(2):
                    ins = pool.tensor_tensor(RTM[:, i, :].rearrange("p (n a w) -> p n a w", a=2, w=w),
                                             W[:, :, :, :, i].rearrange("p n w a -> p n a w"),
                                             y[:, :, i:i + 1, :].to_broadcast([C, D // (2 * w), 2, w]), ALU.mult)
                link(ins)
                ins = pool.tensor_tensor(ROW[:, (s + 1) % 2, :], RTM[:, 0, :], RTM[:, 1, :], ALU.add)
                if s < STAGES - 3:
                    link(ins)
            ins.then_inc(row_folded, 1)

            def rstd1(n):
                lo, hi = LN1[n], LN1[n + 1]
                pool.wait_ge(ln1_stats, n + 1)
                var = MV1[:, 1, lo:hi, :].rearrange("p b u -> p (b u)")
                link(pool.tensor_scalar(var, SUM1[:, 1, 2 * lo:2 * hi], 1.0 / D, EPS, ALU.mult, ALU.add))
                link(pool.tensor_tensor(RS1[:, lo:hi, :].rearrange("p b u -> p (b u)"), var,
                                        POW[:, 0:2 * (hi - lo)], ALU.pow))

            def xn1(b, n):
                if n >= 2:
                    pool.wait_ge(t1_done, b - 1)
                xn = XN[:, n % 2, :, :]
                pool.tensor_tensor(xn, xb(b), MV1[:, 0, one(b), :].rearrange("p o u -> p (o u)").unsqueeze(2)
                                   .to_broadcast([128, 2, D]), ALU.add).then_inc(xc1_ready, 1)
                pool.wait_ge(xc1_ready, b + 1)
                pool.tensor_tensor(xn, xn, RS1[:, one(b), :].rearrange("p o u -> p (o u)").unsqueeze(2)
                                   .to_broadcast([128, 2, D]), ALU.mult).then_inc(xn1_ready, 1)

            rstd1(0)
            xn1(0, 0)
            mean1(1)

            pool.wait_ge(col_ready, 1)
            pool.wait_ge(cw_in, 32)
            for i in range(2):
                ins = pool.tensor_tensor(
                    CT[:, i, :].rearrange("p (n a) -> p n a", a=2), CW[:, 0, :, :]
                    .rearrange("p n (a c) -> p n a c", c=2)[:, :, :, i],
                    COL[:, 0:C].rearrange("p (n c) -> p n c", c=2)[:, :, i:i + 1].to_broadcast([128, 2, 2]), ALU.mult)
            link(ins)
            link(pool.tensor_tensor(CT[:, 2, :], CT[:, 0, :], CT[:, 1, :], ALU.add))
            for i in range(2):
                ins = pool.tensor_tensor(
                    CT[:, i, :].rearrange("p (a n) -> p n a", a=2), CW[:, 1, :, :]
                    .rearrange("p n (a c) -> p n a c", c=2)[:, :, :, i],
                    CT[:, 2, :].rearrange("p (c n) -> p n c", c=2)[:, :, i:i + 1].to_broadcast([128, 2, 2]), ALU.mult)
            link(ins)
            link(pool.tensor_tensor(CT[:, 2, :], CT[:, 0, :], CT[:, 1, :], ALU.add))
            pool.tensor_tensor(BUP[:, :], CT[:, 2, :], COL[:, 4:8], ALU.add).then_inc(bias_ready, 1)
            pool.tensor_scalar(BQS[:, :], COL[:, 8:9], SCALE, None, ALU.mult).then_inc(bias_ready, 1)
            link(pool.tensor_tensor(BY[:, 0:1], COL[:, 10:11], COL[:, 11:12], ALU.add))
            pool.tensor_scalar(BY[:, 1:2], BY[:, 0:1], 0.5, None, ALU.mult).then_inc(bias_ready, 1)

            xn1(1, 1)
            rstd1(1)
            with pool.Fori(1, B // 4) as it:
                xn1(it * 2, 2)
                xn1(it * 2 + 1, 3)
            rstd1(2)
            with pool.Fori(B // 4, B // 2) as it:
                xn1(it * 2, 2)
                xn1(it * 2 + 1, 3)

            pool.wait_ge(dn_stage, SHARED)
            for n in range(SHARED, STAGES):
                w = 2 ** (STAGES - 1 - n)
                pool.wait_ge(dnw_in[n], 16)
                y = WDT[:, n % 2, HID - 128:HID].rearrange("p (n a w) -> p n a w", a=2, w=w)
                W = BW[:, n, 2 * (HID - 128):2 * HID].rearrange("p (n w a c) -> p n w a c", w=w, a=2, c=2)
                for i in range(2):
                    ins = pool.tensor_tensor(TMP[:, i, :].rearrange("p (n a w) -> p n a w", a=2, w=w),
                                             W[:, :, :, i, :].rearrange("p n w a -> p n a w"),
                                             y[:, :, i:i + 1, :].to_broadcast([128, 128 // (2 * w), 2, w]), ALU.mult)
                link(ins)
                pool.tensor_tensor(WDT[:, (n + 1) % 2, HID - 128:HID], TMP[:, 0, :], TMP[:, 1, :], ALU.add)\
                    .then_inc(dn_chunk, 1)
                pool.wait_ge(dn_chunk, n + 1 - SHARED)

            pool.memset(QS[:, :, :, :].rearrange("p u h t -> p (u h t)").bitcast(F32), 0.0).then_inc(fills, 1)
            link(pool.memset(VS[:, :, :, :, :], 0.0))
            for par in range(2):
                at = VW // 2 * par + DH
                ins = pool.memset(VS[64 * par:64 * par + 64, :, :, :, at:at + 1]
                                  .rearrange("p b a j w -> p (b a j) w"), 1.0)
            link(ins)

            def rstd2(b):
                pool.wait_ge(mv2_ready, b + 1)
                pool.tensor_tensor(VE[:, :], MV[:, :, 1], EPSC[:, :], ALU.add).then_inc(ve2_ready, 1)
                pool.wait_ge(ve2_ready, b + 1)
                pool.tensor_tensor(RS[:, :], VE[:, :], POW[:, 0:2], ALU.pow).then_inc(rs2_ready, 1)

            def split_max(g, t):
                nm = NM[:, :, :].rearrange("p a j -> p (a j)")
                pool.wait_ge(nm_ready, t + 1)
                if g >= 1:
                    pool.wait_ge(mt_done, t)
                pool.tensor_tensor(MP[:, 0, :], nm, ZC[:, :], ALU.add).then_inc(mp1, 1)
                pool.wait_ge(mp1, t + 1)
                pool.tensor_tensor(NR[:, :], nm, MP[:, 0, :], ALU.subtract).then_inc(mp2, 1)
                pool.wait_ge(mp2, t + 1)
                pool.tensor_tensor(MP[:, 1, :], NR[:, :], ZC[:, :], ALU.add).then_inc(mp3, 1)
                pool.wait_ge(mp3, t + 1)
                pool.tensor_tensor(MP[:, 2, :], NR[:, :], MP[:, 1, :], ALU.subtract).then_inc(mp_ready, 1)

            def half2(b, n):
                if n + 2 < B:
                    rstd2(b + 2)
                if n == B - 1:
                    split_max(0, 0)
                    split_max(1, 1)
                pool.wait_ge(part1_done, b + 1)
                if n >= 2:
                    pool.wait_ge(part3_done, b - 1)
                pool.tensor_tensor(RES[:, n % 2, :, :], QKF[:, n % 2, :, :], part(b, 0), ALU.subtract)\
                    .then_inc(res_ready, 1)
                if n < 2:
                    k_ones(pool, slice(2 + n, 3 + n))

            rstd2(0)
            rstd2(1)
            batches(pool, half2)

            def rstd3(b):
                pool.wait_ge(mv3_ready, b + 1)
                pool.tensor_tensor(VE[:, :], MV[:, :, 1], EPSC[:, :], ALU.add).then_inc(ve3_ready, 1)
                pool.wait_ge(ve3_ready, b + 1)
                pool.tensor_tensor(RS[:, :], VE[:, :], POW[:, 0:2], ALU.pow).then_inc(rs3_ready, 1)

            def step(s, t, it):
                b = s // 2
                if s + 2 < UNITS:
                    split_max(s + 2, t + 2)
                if s % 2 == 0 and s >= 4:
                    rstd3(2 * it + (s - 4) // 2)
                if s % 2 == 0 and 0 <= b < B:
                    if b >= 2:
                        pool.wait_ge(pv_done, t - 2)
                    pool.tensor_tensor(HOLDP[:, :], ZC[:, 0:1], ZC[:, 0:1], ALU.add)
                    n = H // 2 * J
                    pool.tensor_tensor(VS[:, b % 2, :, :, :].rearrange("p a j (c w) -> p (a j) c w", c=2)[:, :, :, 0:DH],
                                       VA[:, one(2 * it + b), :].rearrange("p o (n d) -> p (o n) d", d=DH)
                                       .unsqueeze(2).to_broadcast([128, n, 2, DH]),
                                       OWN[:, :].unsqueeze(1).unsqueeze(3).to_broadcast([128, n, 2, DH]),
                                       ALU.mult).then_inc(vs_ready, 1)

            pool.wait_ge(vb_ready, B)
            pool.wait_ge(own_ready, 2)
            steps(pool, step)

        @block.scalar
        def _(act):
            act.dma_start(ROW[:, 0, :], b_exp.rearrange("(c n) -> c n", c=C)).then_inc(row_in, 16)
            act.dma_start(RW[:, :, :], up_flat[0:STAGES - 2].rearrange("s (c n) -> c s n", c=C))\
                .then_inc(row_in, 16)
            act.dma_start(WDN[:, :, :], W_con.rearrange("(c p) e -> p c e", p=128)).then_inc(wcon_in, 16)
            act.dma_start(RCOL[0:C, :], up_b.rearrange("(c n) -> c n", c=C)).then_inc(rcol_in, 16)
            for n, v in ((4, bQ), (5, bK)):
                act.dma_start(RCOL[n:n + 1, :].rearrange("o (d h) -> o d h", h=H),
                              v.rearrange("(o h d) -> o d h", o=1, h=H),
                              allow_slow_non_contiguous=True).then_inc(rcol_in, 16)
            for n, v in ((6, b_con), (7, down_b)):
                act.dma_start(RCOL[n:n + 1, :], v.rearrange("(o n) -> o n", o=1)).then_inc(rcol_in, 16)
            for m in range(2):
                act.dma_start(CW[:, m, :, :], up_w[STAGES - 2 + m].rearrange("(n p) a c -> p n (a c)", p=128))\
                    .then_inc(cw_in, 16)

            act.wait_ge(const, CONSTS)
            act.activation(WARM[:, :], POW[:, 0:1], ACT.Gelu)

            junk = HT[:, :, :, :].rearrange("p b c t -> p (b c t)").rearrange("p (n d) -> p n d", d=D)

            def sums1(n):
                act.wait_ge(x_in[n], 16)
                for m in range(n * B, (n + 1) * B):
                    ins = act.activation(junk[:, m, :], X[:, m // 2, m % 2, :], ACT.Copy, accum_out=SUM1[:, 0, m:m + 1])
                ins.then_inc(ln1_sum, 1)

            def squares1(n):
                act.wait_ge(ln1_mean, 1 if n < 2 else 2)
                for m in range(2 * LN1[n], 2 * LN1[n + 1]):
                    ins = act.activation(junk[:, 2 * B + m, :], X[:, m // 2, m % 2, :], ACT.Square,
                                         bias=MV1[:, 0, m // 2, m % 2:m % 2 + 1], accum_out=SUM1[:, 1, m:m + 1])
                ins.then_inc(ln1_stats, 1)

            sums1(0)
            act.wait_ge(wc_t, 1)
            act.activation(WDT[:, 0, :], P[7][:, :], ACT.Copy).then_inc(wdt_ready, 1)
            squares1(0)
            squares1(1)
            act.wait_ge(col_t, 1)
            act.activation(COL[:, 0:12], P[6][:, 0:12], ACT.Copy).then_inc(col_ready, 1)
            sums1(1)

            def gelu(b, c, ps, up_done, gelu_done):
                act.wait_ge(up_done[c], b + 1)
                act.activation(HT[:, one(b), c, :].rearrange("p o t -> p (o t)"), ps[:, 0:S],
                               ACT.Gelu, bias=BUP[:, c:c + 1]).then_inc(gelu_done[c], 1)

            def xnt(b, ps, t_done, ready):
                act.wait_ge(t_done, b + 1)
                act.activation(XNT[:, one(b), :].rearrange("p o t -> p (o t)"), ps[:, 0:S], ACT.Copy)\
                   .then_inc(ready, 1)

            def ys(b, ps, down_done, ready):
                act.wait_ge(down_done, b + 1)
                act.activation(YS[:, :], ps[:, 0:S], ACT.Identity, bias=BY[:, 1:2], scale=0.5)\
                   .then_inc(ready, 1)

            xnt(0, P[0], t1_done, xnt1_ready)
            squares1(2)
            xnt(1, P[0], t1_done, xnt1_ready)
            act.wait_ge(bias_ready, 3)

            def gelus1(b, n):
                gelu(b, 0, P[1], up1_done, gelu1_done)
                gelu(b, 1, P[2], up1_done, gelu1_done)
                if n + 2 < B:
                    xnt(b + 2, P[0], t1_done, xnt1_ready)
                gelu(b, 2, P[3], up1_done, gelu1_done)
                gelu(b, 3, P[4], up1_done, gelu1_done)

            gelus1(0, 0)
            with act.Fori(1, B - 2) as b:
                gelus1(b, 1)
            gelus1(B - 2, B - 2)
            gelus1(B - 1, B - 1)

            act.wait_ge(w_in, 16 * 6)
            for dst, w in ((WQP, WQs), (WKP, WKs)):
                act.activation(dst[:, :].rearrange("k (d h) -> k d h", h=H),
                               w[:, :].rearrange("k (h d) -> k d h", h=H), ACT.Copy).then_inc(wqk_ready, 1)

            def ys1(b, first=False, ps=P[5]):
                if not first:
                    act.wait_ge(yt1_done, b)
                ys(b, ps, down1_done, ys1_ready)

            def xn2t(b, first=False):
                if not first:
                    act.wait_ge(v_done, b)
                act.wait_ge(t2_done, b + 1)
                act.activation(XN2T[:, :], P[0][:, 0:S], ACT.Copy).then_inc(xn2t_ready, 1)

            def qk(b, n):
                if n >= 2:
                    act.wait_ge(res_ready, b - 1)
                if n == 0:
                    act.wait_ge(dn_stage, STAGES)
                    act.wait_ge(dn_chunk, STAGES - SHARED)
                act.wait_ge(qk_done, b + 1)
                for m, (bias, scale) in enumerate(((BQS[:, :], SCALE), (COL[:, 9:10], 1.0))):
                    for dst in (QKF[:, n % 2, m, :], part(b, 0)[:, m, :]):
                        ins = act.activation(dst, P[7][:, m * S:(m + 1) * S], ACT.Identity,
                                             bias=bias, scale=scale)
                ins.then_inc(part1_done, 1)

            def max_t(t):
                act.wait_ge(mt_done, t + 1)
                act.activation(MT[:, :], P[5][0:PARTS * HP * J, 0:64].bitcast(BF16), ACT.Copy)\
                   .then_inc(mts_ready, 1)

            def half2(b, n):
                xn2t(b, n == 0)
                if n + 2 < B:
                    ys1(b + 2)
                qk(b, n)

            ys1(0, True)

            act.activation(IDB[:, :], IDF[:, :], ACT.Copy).then_inc(idb_ready, 1)
            act.wait_ge(tri_ready, 2)
            for par in range(2):
                rows = slice(64 * par, 64 * par + 64)
                for m in range(2):
                    act.activation(MSK[rows, m, :, :], TRI[rows, m, 64 * par:64 * par + 64].unsqueeze(1)
                                   .to_broadcast([64, 4, 64]), ACT.Copy).then_inc(msk_ready, 1)

            ys1(1, ps=P[2])
            batches(act, half2)
            max_t(0)
            max_in(act, 0, 0)

            def exps(g, k, t):
                act.wait_ge(s2_done[k], t)
                act.activation(PX[:, g % 2, k, :], P[2 + bank(g, k)][:, :], ACT.Exp).then_inc(exp_done[k], 1)

            def ffn2(b, n):
                for c in range(C):
                    gelu(b, c, P[c], up3_done, gelu3_done)
                if n >= 1:
                    ys3(b - 1, n == 1)
                if n == 2:
                    xnt(B - 1, P[5][:, S:2 * S], t3_done, xnt3_ready)

            def ys3(b, first=False, ps=P[4]):
                if not first:
                    act.wait_ge(yt3_done, b)
                ys(b, ps, down3_done, ys3_ready)

            def step(s, t, it):
                def ex(k):
                    if 0 <= s < UNITS:
                        exps(s, k, t + 1)

                if 0 <= s < UNITS and s >= 2:
                    act.wait_ge(pv_done, t - 1)
                ex(0)
                if s + 1 < UNITS:
                    act.wait_ge(m_in[s % 4], (it + (s // 4 + 1)) * 32)
                    max_t(t + 1)
                ex(1)
                ex(2)
                ex(3)
                b = (s - 5) // 2
                if s % 2 and b >= 0:
                    xnt(2 * it + b, P[5][:, S:2 * S], t3_done, xnt3_ready)
                b = (s - 3) // 2
                if s % 2 and 0 <= b < B:
                    act.wait_ge(zt_done, 2 * it + (b + 1))
                    if b >= 1:
                        act.wait_ge(wo_done, 2 * it + b)
                    act.activation(ZT[0:DH, :], P[7][0:DH, 0:S], ACT.Copy).then_inc(zts_ready, 1)
                if s == UNITS:
                    ffn2(0, 0)
                if 0 <= s - 1 < UNITS:
                    act.wait_ge(pv_done, t)
                    if s >= 2:
                        act.wait_ge(ott_done, t - 1)
                    act.activation(OT[:, :], P[4][:, 0:S], ACT.Copy).then_inc(ot_ready, 1)
                ex(4)
                if s > UNITS:
                    ffn2(s - UNITS, s - UNITS)

            steps(act, step)

            with act.Fori(3, B - 1) as b:
                ffn2(b, 3)
            ffn2(B - 1, B - 1)
            ys3(B - 1, ps=P[7])

        @block.vector
        def _(dve):
            chain = [0]

            def link(ins):
                chain[0] += 1
                ins.then_inc(dve_chain, 1)
                dve.wait_ge(dve_chain, chain[0])

            link(dve.memset(OWN[:, :], 0.0))
            for par in range(2):
                dve.memset(OWN[64 * par:64 * par + 64, par:par + 1], 1.0).then_inc(own_ready, 1)

            def stage(W, y, o, w, transposed, done, cols=HID):
                W, y, o = W[:, 0:2 * cols], y[:, 0:cols], o[:, 0:cols]
                yv = y.rearrange("p (n a w) -> p n a w", a=2, w=w)
                Wv = W.rearrange("p (n w a c) -> p n w a c", w=w, a=2, c=2)
                for i in range(2):
                    wv = Wv[:, :, :, :, i].rearrange("p n w a -> p n a w") if not transposed else \
                        Wv[:, :, :, i, :].rearrange("p n w a -> p n a w")
                    ins = dve.tensor_tensor(TM[:, i, 0:cols].rearrange("p (n a w) -> p n a w", a=2, w=w), wv,
                                            yv[:, :, i:i + 1, :].to_broadcast([128, cols // (2 * w), 2, w]), ALU.mult)
                link(ins)
                ins = dve.tensor_tensor(o, TM[:, 0, 0:cols], TM[:, 1, 0:cols], ALU.add)
                done(ins)

            dve.wait_ge(wup_in, 16)
            for s in range(STAGES):
                dve.wait_ge(upw_in[s], 16)

                def done(ins):
                    ins.then_inc(up_stage, 1)
                    dve.wait_ge(up_stage, s + 1)
                stage(BW[:, s, :], WUP[:, s % 2, :], WUP[:, (s + 1) % 2, :], 2 ** s, False, done)
            dve.wait_ge(wdt_ready, 1)
            for n in range(STAGES):
                dve.wait_ge(dnw_in[n], 16)

                def done(ins):
                    ins.then_inc(dn_stage, 1)
                    dve.wait_ge(dn_stage, n + 1)
                stage(BW[:, n, :], WDT[:, n % 2, :], WDT[:, (n + 1) % 2, :], 2 ** (STAGES - 1 - n), True, done,
                      HID if n < SHARED else HID - 128)
            dve.wait_ge(wdn_t, 1)
            dve.tensor_copy(WDN[:, :, :].rearrange("p c e -> p (c e)"), P[7][:, :]).then_inc(wdn_ready, 1)

            dve.wait_ge(w_in, 16 * 6)

            def stats(b, st_done, mv_done):
                for u in range(2):
                    ins = dve.bn_stats(ST[:, u, :], X[:, one(b), u, :].rearrange("p o d -> p (o d)"))
                ins.then_inc(st_done, 1)
                dve.wait_ge(st_done, b + 1)
                dve.memset(HOLD[:, :], 0.0)
                for u in range(2):
                    ins = dve.bn_aggr(MV[:, u, :], ST[:, u, :])
                ins.then_inc(mv_done, 1)

            def normalise(b, n, rs_ready, left, ready):
                if n >= 2:
                    dve.wait_ge(left, b - 1)
                dve.wait_ge(rs_ready, b + 1)
                for u in range(2):
                    ins = dve.tensor_scalar(XN[:, n % 2, u, :], X[:, one(b), u, :].rearrange("p o d -> p (o d)"),
                                            MV[:, u, 0:1], RS[:, u:u + 1], ALU.subtract, ALU.mult)
                ins.then_inc(ready, 1)

            def x1_stats(b):
                dve.wait_ge(yt1_done, b + 1)
                dve.tensor_tensor(xb(b), xb(b), P[6][:, 0:S].rearrange("p (u d) -> p u d", u=2), ALU.add)\
                   .then_inc(x1_done, 1)
                dve.wait_ge(x1_done, b + 1)
                dve.memset(HOLD[:, :], 0.0)
                stats(b, st2, mv2_ready)

            def v_blocks(b):
                dve.wait_ge(v_done, b + 1)
                dve.tensor_tensor(VA[:, one(b), :].rearrange("p o (a j d) -> p (o a) j d", j=J, d=DH),
                                  P[1][:, 0:S].rearrange("p (j a d) -> p a j d", j=J, d=DH),
                                  BVP[:, :].rearrange("p (a d) -> p a d", d=DH).unsqueeze(2)
                                  .to_broadcast([128, H // 2, J, DH]), ALU.add).then_inc(vb_ready, 1)

            def parts(b, n):
                dve.wait_ge(res_ready, b + 1)
                dve.tensor_copy(part(b, 1), RES[:, n % 2, :, :]).then_inc(part2_done, 1)
                dve.wait_ge(part2_done, b + 1)
                dve.tensor_tensor(part(b, 2), RES[:, n % 2, :, :], part(b, 1), ALU.subtract)\
                   .then_inc(part3_done, 1)

            for par in range(2):
                rows = slice(64 * par, 64 * par + 64)
                ins = dve.tensor_copy(
                    BVP[rows, :].rearrange("p (f n) -> p f n", f=2),
                    BV[rows, :].rearrange("p (f c n) -> p f c n", f=2, c=2)[:, :, par, :])
            link(ins)

            k_ones(dve, slice(0, 2))

            def maxima(g, k, t):
                dve.wait_ge(s1_done[k], t)
                dve.tensor_reduce(PM[:, g % 2, k, :], P[max_bank(g, k)][:, :].rearrange("p (n w) -> p n w", w=64),
                                  AX.X, ALU.max).then_inc(max_done[k], 1)

            def neg_max(g, t):
                if g >= 1:
                    dve.wait_ge(mp2, t)
                dve.wait_ge(max_done[4], t + 1)
                pm = PM[:, g % 2, :, :]
                for j, of in ((3, pm[:, 0:HP, 0:4]), (0, pm[:, 0:HP, 4:5]), (2, pm[:, 0:HP, 5:8]),
                              (1, pm[:, HP, :].rearrange("p (a j) -> p a j", j=2))):
                    ins = dve.tensor_reduce(NM[:, :, j], of, AX.X, ALU.max, negate=True)
                ins.then_inc(nm_ready, 1)

            def norm2(b, n):
                normalise(b, n, rs2_ready, t2_done, xn2_ready)

            def half2(b, n):
                v_blocks(b)
                if n + 2 < B:
                    x1_stats(b + 2)
                if 1 <= n < B - 2:
                    parts(b - 1, n - 1)
                if n + 2 < B:
                    norm2(b + 2, n + 2)

            def first_maxima():
                for k in range(5):
                    maxima(0, k, 1)
                neg_max(0, 0)
                maxima(1, 0, 2)
                maxima(1, 1, 2)
                v_blocks(B - 1)
                for k in range(2, 5):
                    maxima(1, k, 2)
                neg_max(1, 1)
                parts(B - 3, B - 3)

            for n in range(2):
                x1_stats(n)
                norm2(n, n)
            batches(dve, half2, first_maxima)

            def stats3(b):
                dve.wait_ge(x2_done, b + 1)
                dve.memset(HOLD[:, :], 0.0)
                stats(b, st3, mv3_ready)

            def result(b):
                dve.wait_ge(yt3_done, b + 1)
                dve.tensor_tensor(xb(b), xb(b), P[6][:, 0:S].rearrange("p (u d) -> p u d", u=2), ALU.add)\
                   .then_inc(out_ready, 1)

            def step(s, t, it):
                def mx(k):
                    if 0 <= s + 2 < UNITS:
                        maxima(s + 2, k, t + 3)

                mx(0)
                b = (s - 4) // 2
                if s % 2 == 0 and 0 <= b < B:
                    dve.wait_ge(wo_done, 2 * it + (b + 1))
                    x = xb(2 * it + b)
                    dve.tensor_tensor(x, x, P[7][:, S:2 * S].rearrange("p (u d) -> p u d", u=2), ALU.add)\
                       .then_inc(x2_done, 1)
                if s < 2:
                    parts(B - 2 + s, B - 2 + s)
                mx(1)
                b = (s - 5) // 2
                if s % 2 and b >= 0:
                    normalise(2 * it + b, b % 2, rs3_ready, t3_done, xn3_ready)
                mx(2)
                g = s - 2
                if 0 <= g < UNITS:
                    dve.wait_ge(ott_done, t - 1)
                    o = P[6][:, 0:2 * 128].rearrange("p (n w) -> p n w", w=VW // 2)
                    dve.reciprocal(RD[:, :], o[:, :, DH]).then_inc(rd_ready, 1)
                    dve.wait_ge(rd_ready, t - 1)
                    at = HH * (g % 2)
                    dve.tensor_tensor(ZH[:, :, :, at:at + HH].rearrange("p u d h -> p u h d"),
                                      P[6][:, 0:2 * 128].rearrange("p (u h w) -> p u h w", u=2, w=VW // 2)[:, :, :, 0:DH],
                                      RD[:, :].rearrange("p (u h) -> p u h", u=2).unsqueeze(3)
                                      .to_broadcast([128, 2, HH, DH]), ALU.mult).then_inc(zh_ready, 1)
                    if g % 2:
                        dve.wait_ge(zh_ready, t - 1)
                        if g >= 2:
                            dve.wait_ge(zt_done, 2 * it + g // 2)
                        dve.tensor_reduce(Z[:, :, :].rearrange("p u d -> p (u d)"),
                                          ZH[:, :, :, :].rearrange("p u d h -> p (u d) h"),
                                          AX.X, ALU.add).then_inc(z_ready, 1)
                mx(3)
                mx(4)
                if s + 2 < UNITS:
                    neg_max(s + 2, t + 2)
                if s % 2 == 0 and s >= 4:
                    stats3(2 * it + (s - 4) // 2)
                if s == UNITS + 2:
                    normalise(B - 1, B - 1, rs3_ready, t3_done, xn3_ready)
                    result(0)

            steps(dve, step)

            with dve.Fori(1, B) as b:
                result(b)

        @block.tensor
        def _(pe):
            pe.wait_ge(id_ready, 1)
            pe.wait_ge(wcon_in, 16)
            for c in range(C):
                ins = pe.transpose(P[7][:, c * 128:(c + 1) * 128], WDN[:, c, :], IDF[:, :])
            ins.then_inc(wc_t, 1)
            pe.wait_ge(rcol_in, 16 * 5)
            pe.wait_ge(row_folded, 1)
            pe.transpose(P[6][:, 0:C], ROW[:, (STAGES - 2) % 2, :], IDF[0:C, 0:C])
            pe.transpose(P[6][:, C:C + 8], RCOL[:, :], IDF[0:8, 0:8]).then_inc(col_t, 1)

            def t_x(b, ps, ready, left, done, first, slot):
                pe.wait_ge(ready, b + 1)
                if not first:
                    pe.wait_ge(left, b)
                for u in range(2):
                    ins = pe.transpose(ps[:, u * 128:(u + 1) * 128], XN[:, slot, u, :], IDF[:, :])
                ins.then_inc(done, 1)

            def up(b, c, ps, ready, gelu_done, done, first=False):
                if c == 0:
                    pe.wait_ge(ready, b + 1)
                if not first:
                    pe.wait_ge(gelu_done[c], b)
                pe.matmul(ps[:, 0:S], WUP[:, STAGES % 2, c * 128:(c + 1) * 128],
                          XNT[:, one(b), :].rearrange("p o t -> p (o t)"), start=True, stop=True)\
                  .then_inc(done[c], 1)

            def down(b, ps, gelu_done, ys_ready, done, first=False, chunks=range(C)):
                if not first:
                    pe.wait_ge(ys_ready, b)
                for c in chunks:
                    pe.wait_ge(gelu_done[c], b + 1)
                    ins = pe.matmul(ps[:, 0:S], WDN[:, c, :],
                                    HT[:, one(b), c, :].rearrange("p o t -> p (o t)"),
                                    start=c == 0, stop=c == C - 1)
                if C - 1 in chunks:
                    ins.then_inc(done, 1)

            def t_y(b, ys_ready, left, done, first=False):
                pe.wait_ge(ys_ready, b + 1)
                if not first:
                    pe.wait_ge(left, b)
                for u in range(2):
                    ins = pe.transpose(P[6][:, u * 128:(u + 1) * 128], YS[:, u * 128:(u + 1) * 128], IDF[:, :])
                ins.then_inc(done, 1)

            def up1(b, c, first=False):
                up(b, c, P[1 + c], xnt1_ready, gelu1_done, up1_done, first)

            def t_x1(b, n):
                t_x(b, P[0], xn1_ready, xnt1_ready, t1_done, n == 0, n % 2)

            def half1(b, n):
                up1(b, 0, n == 0)
                up1(b, 1, n == 0)
                if n + 2 < B:
                    t_x1(b + 2, n + 2)
                up1(b, 2, n == 0)
                up1(b, 3, n == 0)

            t_x1(0, 0)
            t_x1(1, 1)
            pe.wait_ge(up_stage, STAGES)
            batches(pe, half1)

            pe.wait_ge(dn_stage, STAGES)
            pe.wait_ge(dn_chunk, STAGES - SHARED)
            for c in range(C):
                ins = pe.transpose(P[7][:, c * 128:(c + 1) * 128],
                                   WDT[:, STAGES % 2, c * 128:(c + 1) * 128], IDF[:, :])
            ins.then_inc(wdn_t, 1)
            pe.wait_ge(wdn_ready, 1)

            def t_x2(b, n):
                t_x(b, P[0], xn2_ready, xn2t_ready, t2_done, n == 0, n % 2)

            def qkv(b, first=False):
                pe.wait_ge(xn2t_ready, b + 1)
                if first:
                    pe.wait_ge(wqk_ready, 2)
                if not first:
                    pe.wait_ge(part1_done, b)
                for n, w in enumerate((WQP, WKP)):
                    ins = pe.matmul(P[7][:, n * S:(n + 1) * S], w[:, :], XN2T[:, :], start=True, stop=True)
                ins.then_inc(qk_done, 1)
                if not first:
                    pe.wait_ge(vb_ready, b)
                for j in range(J):
                    for par in range(2):
                        w = WVs[:, :].rearrange("k (f c n) -> k f c n", f=2, c=2)[:, :, par, :]
                        ins = pe.matmul(P[1][64 * par:64 * par + 64, 64 * j:64 * j + 64],
                                        XN2T[:, 64 * j:64 * j + 64], w, start=True, stop=True)
                ins.then_inc(v_done, 1)

            def down1(b, first=False):
                down(b, P[5], gelu1_done, ys1_ready, down1_done, first)

            def t_y1(b, first=False):
                t_y(b, ys1_ready, x1_done, yt1_done, first)

            def mask(ps, m, cols, first):
                n = cols // 64
                return pe.matmul(ps, IDB[:, :], MSK[:, m, 0:n, :], start=first, stop=False, skip_group_check=True)

            def scores_max(g, k, t, it):
                u = g % 4
                ps = P[max_bank(g, k)]
                if k == 0:
                    pe.wait_ge(stack_in[u], (it + (g // 4 + 1)) * 32)
                if k >= 2:
                    pe.wait_ge(max_done[k - 2], t)
                elif g >= 1:
                    pe.wait_ge(max_done[k + 3], t - 1)
                if k < HP:
                    mask(ps[:, 192:320], 0, 128, True)
                    mask(ps[:, 448:512], 0, 64, False)
                    todo = [(j, k, at) for j, at in MAX_AT.items()]
                else:
                    mask(ps[:, :].rearrange("p (a w) -> p a w", w=128)[:, :, 64:128], 0, 256, True)
                    todo = [(1, hp, 128 * hp) for hp in range(HP)]
                for j, hp, at in todo:
                    for par in range(2):
                        h = head(par, hp)
                        ins = pe.matmul(ps[64 * par:64 * par + 64, at:at + 64 * (j + 1)],
                                        QS[:, u, h, 64 * j:64 * j + 64], KS[:, u, h, 0:64 * (j + 1)],
                                        start=False, stop=True, skip_group_check=True)
                ins.then_inc(s1_done[k], 1)

            def max_t(g, t):
                pe.wait_ge(mp_ready, t + 1)
                if g >= 1:
                    pe.wait_ge(mts_ready, t)
                pe.transpose(P[5][:, 0:64].bitcast(BF16),
                             MP[:, :, :].rearrange("p i n -> p (i n)"), IDB[:, :]).then_inc(mt_done, 1)

            def half2(b, n):
                t_x2(b, n)
                if n >= 1 and n + 2 < B:
                    down1(b + 2)
                qkv(b, n == 0)
                if n + 2 < B:
                    t_y1(b + 2)
                if n == B - 2:
                    pe.wait_ge(gelu1_done[C - 1], B)
                    pe.wait_ge(fills, 4)
                    pe.wait_ge(msk_ready, 4)
                    pe.wait_ge(idb_ready, 1)
                    scores_max(0, 0, 1, 0)
                    scores_max(0, 1, 1, 0)

            def first_scores():
                t_x2(B - 1, B - 1)
                for k in range(2, 5):
                    scores_max(0, k, 1, 0)
                qkv(B - 1)
                scores_max(1, 0, 2, 0)
                scores_max(1, 1, 2, 0)
                max_t(0, 0)
                for k in range(2, 5):
                    scores_max(1, k, 2, 0)

            down1(0, True)
            pe.wait_ge(gelu1_done[1], B)
            down(1, P[2], gelu1_done, ys1_ready, down1_done, True, range(C // 2))
            t_y1(0, True)
            down(1, P[2], gelu1_done, ys1_ready, down1_done, True, range(C // 2, C))
            pe.wait_ge(ys1_ready, 1)
            down(2, P[5], gelu1_done, ys1_ready, down1_done, True)
            t_y1(1)
            batches(pe, half2, first_scores)

            pe.wait_ge(vb_ready, B)

            def scores_exp(g, k, t, it):
                u = g % 4
                ps = P[2 + bank(g, k)]
                if k == 0:
                    pe.wait_ge(m_in[u], (it + (g // 4 + 1)) * 32)
                    if g == 0:
                        pe.wait_ge(max_done[4], 2)
                if k >= 2:
                    pe.wait_ge(exp_done[k - 2], t)
                elif g >= 1:
                    pe.wait_ge(exp_done[k + 3], t - 1)
                if k < HP:
                    mask(ps[:, 0:128], 1, 128, True)
                    mask(ps[:, 320:384], 1, 64, False)
                    todo = [(i, k, at) for i, at in EXP_AT.items()]
                else:
                    mask(ps[:, :].rearrange("p (a w) -> p a w", w=128)[:, :, 0:64], 1, 256, True)
                    todo = [(2, hp, 128 * hp) for hp in range(HP)]
                for i, hp, at in todo:
                    for par in range(2):
                        h = head(par, hp)
                        ins = pe.matmul(ps[64 * par:64 * par + 64, at:at + S - 64 * i],
                                        KS[:, u, h, 64 * i:64 * i + 64],
                                        QS[:, u, h, 64 * i:S],
                                        start=False, stop=True, skip_group_check=True)
                ins.then_inc(s2_done[k], 1)

            def pv(g, t, it):
                pe.wait_ge(exp_done[4], t)
                if g % 2 == 0:
                    pe.wait_ge(vs_ready, 2 * it + (g // 2 + 1))
                if g >= 1:
                    pe.wait_ge(ot_ready, t - 1)
                for i in range(J):
                    for hp in range(HP):
                        px = PX[:, g % 2, 4, 128 * hp:128 * hp + 128] if i == 2 else \
                            PX[:, g % 2, hp, EXP_AT[i]:EXP_AT[i] + S - 64 * i]
                        ins = pe.matmul(P[4][VW * hp:VW * (hp + 1), 64 * i:S],
                                        VS[:, g // 2 % 2, HP * (g % 2) + hp, i, :], px,
                                        start=i == 0, stop=i == J - 1)
                ins.then_inc(pv_done, 1)

            def t_x3(b, n):
                t_x(b, P[5][:, S:2 * S], xn3_ready, xnt3_ready, t3_done, n == 0, n % 2)

            def down3(b, first=False):
                down(b, P[4], gelu3_done, ys3_ready, down3_done, first)

            def t_y3(b, first=False):
                t_y(b, ys3_ready, out_ready, yt3_done, first)

            def up3(b, n, chunks):
                for c in chunks:
                    up(b, c, P[c], xnt3_ready, gelu3_done, up3_done, n == 0)

            def ffn2(b, n):
                up3(b, n, range(0, 2))
                if n >= 2:
                    t_y3(b - 2, n == 2)
                up3(b, n, range(2, 4))
                if n >= 1:
                    down3(b - 1, n == 1)

            def step(s, t, it):
                def s1(k):
                    if 0 <= s + 2 < UNITS:
                        scores_max(s + 2, k, t + 3, it)

                def s2(k):
                    if 0 <= s < UNITS:
                        scores_exp(s, k, t + 1, it)

                if s == UNITS - 1:
                    pe.wait_ge(max_done[4], UNITS)
                    up3(0, 0, range(0, 2))
                s1(0)
                s2(0)
                s1(1)
                s2(1)
                if s + 1 < UNITS:
                    b = (s - 6) // 2
                    if s % 2 == 0 and b >= 0:
                        pe.wait_ge(xnt3_ready, 2 * it + (b + 1))
                    max_t(s + 1, t + 1)
                if 0 <= s - 2 < UNITS:
                    pe.wait_ge(ot_ready, t - 1)
                    if s - 2 >= 1:
                        pe.wait_ge(zh_ready, t - 2)
                    for u in range(2):
                        ins = pe.transpose(P[6][:, u * 128:(u + 1) * 128], OT[:, u * 128:(u + 1) * 128], IDF[:, :])
                    ins.then_inc(ott_done, 1)
                s1(2)
                s2(2)
                s1(3)
                s2(3)
                s1(4)
                b = (s - 5) // 2
                if s % 2 and b >= 0:
                    if s < UNITS - 1:
                        pe.wait_ge(mts_ready, t + 2)
                    t_x3(2 * it + b, b)
                if s == UNITS:
                    pe.wait_ge(exp_done[4], UNITS)
                    up3(0, 0, range(2, 4))
                b = (s - 3) // 2
                has_z = s % 2 and 0 <= b < B
                if has_z:
                    pe.wait_ge(z_ready, 2 * it + (b + 1))
                    for u in range(2):
                        ins = pe.transpose(P[7][0:DH, u * 128:(u + 1) * 128], Z[:, u, :], IDF[:, :])
                    ins.then_inc(zt_done, 1)
                if s == UNITS + 1:
                    up3(1, 1, range(2, 4))
                if 0 <= s - 1 < UNITS:
                    pv(s - 1, t, it)
                if s == UNITS:
                    up3(1, 1, range(0, 2))
                s2(4)
                if has_z:
                    pe.wait_ge(zts_ready, 2 * it + (b + 1))
                    if b >= 1:
                        pe.wait_ge(x2_done, 2 * it + b)
                    for u in range(2):
                        ins = pe.matmul(P[7][:, S + u * 128:S + (u + 1) * 128], ZT[:, u * 128:(u + 1) * 128],
                                        WOs[:, :], start=True, stop=True)
                    ins.then_inc(wo_done, 1)
                if s == UNITS + 1:
                    pe.wait_ge(ot_ready, UNITS)
                    down3(0, True)
                if s == UNITS + 2:
                    pe.wait_ge(zh_ready, UNITS)
                    ffn2(2, 2)
                    t_x3(B - 1, B - 1)

            steps(pe, step)

            with pe.Fori(3, B - 1) as b:
                ffn2(b, 3)
            ffn2(B - 1, B - 1)
            down(B - 1, P[7], gelu3_done, ys3_ready, down3_done, True)
            t_y3(B - 2)
            t_y3(B - 1)


_INS = ["x", "WQ", "bQ", "WK", "bK", "WV", "bV", "WO", "bO"]
_FFN = ["W_exp", "b_exp", "up_weights", "up_bias", "down_weights", "W_con", "b_con", "down_bias"]


def kernel(**inputs):
    import numpy as np
    import concourse.bacc as bacc
    from concourse import mybir as mb
    from concourse.bass_utils import run_bass_kernel_spmd as run

    nc = bacc.Bacc("TRN2", target_bir_lowering=False, num_devices=1)
    arrays, args = {}, []
    for name in ["L0_attn_" + n for n in _INS] + ["L0_ffn_" + n for n in _FFN]:
        a = np.ascontiguousarray(inputs[name])
        arrays[name] = a
        args.append(nc.dram_tensor(name, a.shape, mb.dt.from_np(a.dtype), kind="ExternalInput").ap())
    out = nc.dram_tensor("out", (B, S, D), F32, kind="ExternalOutput").ap()
    build(nc, *args, out)
    return run(nc, [arrays], core_ids=[0]).results[0]["out"]
```
